# Optimizing a Trainium2 kernel written in Bass

```python
import numpy as np
import jax
import jax.numpy as jnp

def _softmax(x, axis=-1):
    return jax.nn.softmax(x, axis=axis)

def _gelu(x):
    return jax.nn.gelu(x, approximate=True)

def _silu(x):
    return jax.nn.silu(x)

def _sigmoid(x):
    return jax.nn.sigmoid(x)

def _layernorm(x, axis=-1, eps=1e-05):
    m = jnp.mean(x, axis=axis, keepdims=True)
    v = jnp.var(x, axis=axis, keepdims=True)
    return (x - m) / jnp.sqrt(v + eps)

def _scatter_add(tgt, idx, src, axis=0):
    return tgt.at[idx].add(src)

def _segment_sum(src, seg, n):
    return jax.ops.segment_sum(src, seg, n)
kernel_name = 'mk_gnn_resnorm_d2_gnn_r8_7e9587'

def setup_inputs(seed: int=0):
    np.random.seed(seed)
    _w = jnp.asarray

    def _rec_inputs():
        import jax
        import jax.numpy as jnp
        _gk = jax.random.key(seed)
        x = -0.0001006 + 1 * jax.random.normal(jax.random.fold_in(_gk, 1), (12500, 96), jnp.float32)
        _s = jax.random.randint(jax.random.fold_in(_gk, 2), (100000,), 0, 12500, jnp.int32)
        _d = jax.random.randint(jax.random.fold_in(_gk, 3), (100000,), 0, 12500, jnp.int32)
        _loop = jnp.arange(12500, dtype=jnp.int32)
        src = jnp.concatenate([_s, _d, _loop])
        dst = jnp.concatenate([_d, _s, _loop])
        _o = jnp.argsort(dst, stable=True)
        src = src[_o]
        dst = dst[_o]
        edge_attr_96 = 5.93493e-05 + 1.00006 * jax.random.normal(jax.random.fold_in(_gk, 12), (212500, 96), jnp.float32)
        return (x, src, dst, edge_attr_96)
    x, src, dst, edge_attr_96 = _rec_inputs()

    def _L0_gnn_setup():
        import jax, jax.numpy as jnp
        import numpy as np
        EPS = 1e-07
        BETA = 1.0
        key = jax.random.key(seed)
        k1, k2, k3, k4 = jax.random.split(key, 4)
        N, E, D_IN, D_OUT = (6250, 100000, 96, 96)
        feat = jax.random.normal(k1, (N, D_IN), dtype=jnp.float32)
        src = jax.random.randint(k2, (E,), 0, N, dtype=jnp.int32)
        dst = jax.random.randint(k3, (E,), 0, N, dtype=jnp.int32)
        W = jax.random.normal(k4, (D_IN, D_OUT), dtype=jnp.float32) / np.sqrt(D_IN)
        b = jnp.zeros((D_OUT,), dtype=jnp.float32)
        return {'feat': feat, 'src': src, 'dst': dst, 'W': W, 'b': b}
    _L0_gnn_all = _L0_gnn_setup()
    _L0_gnn_in = {k: v for k, v in _L0_gnn_all.items() if k in ('W', 'b')}
    del _L0_gnn_all

    def _L1_gnn_setup():
        import jax, jax.numpy as jnp
        import numpy as np
        N_NODES = 6250
        N_EDGES = 100000
        IN_DIM = 96
        NUM_HEADS = 8
        HEAD_DIM = IN_DIM // NUM_HEADS
        key = jax.random.key(seed)
        ks = jax.random.split(key, 11)
        s = 1.0 / np.sqrt(IN_DIM)
        return {'x': jax.random.normal(ks[0], (N_NODES, IN_DIM), dtype=jnp.float32), 'edge_index': jax.random.randint(ks[1], (2, N_EDGES), 0, N_NODES, dtype=jnp.int64), 'edge_attr': jax.random.normal(ks[2], (N_EDGES, IN_DIM), dtype=jnp.float32), 'Wq': jax.random.normal(ks[3], (IN_DIM, IN_DIM), dtype=jnp.float32) * s, 'bq': jax.random.normal(ks[4], (IN_DIM,), dtype=jnp.float32) * s, 'Wk': jax.random.normal(ks[5], (IN_DIM, IN_DIM), dtype=jnp.float32) * s, 'bk': jax.random.normal(ks[6], (IN_DIM,), dtype=jnp.float32) * s, 'We': jax.random.normal(ks[7], (IN_DIM, IN_DIM), dtype=jnp.float32) * s, 'be': jax.random.normal(ks[8], (IN_DIM,), dtype=jnp.float32) * s, 'Wv': jax.random.normal(ks[9], (IN_DIM, IN_DIM), dtype=jnp.float32) * s, 'bv': jax.random.normal(ks[10], (IN_DIM,), dtype=jnp.float32) * s}
    _L1_gnn_all = _L1_gnn_setup()
    _L1_gnn_in = {k: v for k, v in _L1_gnn_all.items() if k in ('Wq', 'bq', 'Wk', 'bk', 'We', 'be', 'Wv', 'bv')}
    del _L1_gnn_all
    return {'x': x, 'src': src, 'dst': dst, 'edge_attr_96': edge_attr_96, 'L0_gnn_W': _L0_gnn_in['W'], 'L0_gnn_b': _L0_gnn_in['b'], 'L1_gnn_Wq': _L1_gnn_in['Wq'], 'L1_gnn_bq': _L1_gnn_in['bq'], 'L1_gnn_Wk': _L1_gnn_in['Wk'], 'L1_gnn_bk': _L1_gnn_in['bk'], 'L1_gnn_We': _L1_gnn_in['We'], 'L1_gnn_be': _L1_gnn_in['be'], 'L1_gnn_Wv': _L1_gnn_in['Wv'], 'L1_gnn_bv': _L1_gnn_in['bv']}

def reference(x, src, dst, edge_attr_96, L0_gnn_W, L0_gnn_b, L1_gnn_Wq, L1_gnn_bq, L1_gnn_Wk, L1_gnn_bk, L1_gnn_We, L1_gnn_be, L1_gnn_Wv, L1_gnn_bv):
    import jax
    import jax.numpy as jnp

    def _L0_gnn_ref(feat, src, dst, W, b):
        import jax, jax.numpy as jnp
        import numpy as np
        EPS = 1e-07
        BETA = 1.0
        N = feat.shape[0]
        m = jax.nn.relu(feat[src]) + EPS
        logits = BETA * m
        seg_max = jax.ops.segment_max(logits, dst, num_segments=N)
        ex = jnp.exp(logits - seg_max[dst])
        denom = jax.ops.segment_sum(ex, dst, num_segments=N)
        a = ex / denom[dst]
        msg = jax.ops.segment_sum(a * m, dst, num_segments=N)
        feats = feat + msg
        return feats @ W + b

    def _L1_gnn_ref(x, edge_index, edge_attr, Wq, bq, Wk, bk, We, be, Wv, bv):
        import jax, jax.numpy as jnp
        import numpy as np
        N_NODES = 6250
        N_EDGES = 100000
        IN_DIM = 96
        NUM_HEADS = 8
        HEAD_DIM = IN_DIM // NUM_HEADS
        N = x.shape[0]
        H, D = (NUM_HEADS, HEAD_DIM)
        Q_h = (x @ Wq + bq).reshape(N, H, D)
        K_h = (x @ Wk + bk).reshape(N, H, D)
        V_h = (x @ Wv + bv).reshape(N, H, D)
        E = (edge_attr @ We + be).reshape(-1, H, D)
        src_idx = edge_index[0]
        dst_idx = edge_index[1]
        src = K_h[src_idx]
        dest = Q_h[dst_idx]
        score = src * dest / jnp.sqrt(jnp.asarray(D, x.dtype))
        score = score * E
        score = jnp.exp(jnp.clip(score.sum(-1, keepdims=True), -5.0, 5.0))
        msg = V_h[src_idx] * score
        wV = jax.ops.segment_sum(msg, dst_idx, num_segments=N)
        Z = jax.ops.segment_sum(score, dst_idx, num_segments=N)
        h_out = wV / (Z + 1e-06)
        return h_out.reshape(N, H * D)
    edge_index = jnp.stack([src, dst])
    x = _layernorm(x + _L0_gnn_ref(x, src, dst, L0_gnn_W, L0_gnn_b), axis=-1)
    x = _layernorm(x + _L1_gnn_ref(x, edge_index, edge_attr_96, L1_gnn_Wq, L1_gnn_bq, L1_gnn_Wk, L1_gnn_bk, L1_gnn_We, L1_gnn_be, L1_gnn_Wv, L1_gnn_bv), axis=-1)
    return x

_drawn_inputs = setup_inputs


def setup_inputs(seed=0):
    import zlib

    import numpy as np

    out = dict(_drawn_inputs(seed))
    spreads = {'L0_gnn_b': (0.0, 0.1)}
    factors = {}
    for name, (base, spread) in spreads.items():
        noise = np.random.default_rng([zlib.crc32(name.encode()), seed]).standard_normal(out[name].shape)
        drawn = base * np.exp(spread * noise) if base else spread * noise
        out[name] = jnp.asarray(drawn.astype(out[name].dtype))
    for name, factor in factors.items():
        out[name] = (out[name] * factor).astype(out[name].dtype)
    return out
```

```python
from contextlib import ExitStack

import concourse.bass as bass
from concourse import mybir
from concourse.alu_op_type import AluOpType as ALU

FP32 = mybir.dt.float32
I32 = mybir.dt.int32
U16 = mybir.dt.uint16
BF16 = mybir.dt.bfloat16
ACT = mybir.ActivationFunctionType
AX = mybir.AxisListType
DVE_ENGINE = mybir.EngineType.DVE
PE_ENGINE = mybir.EngineType.PE
SP_ENGINE = mybir.EngineType.SP

P = 128
NODES, EDGES, D, HEADS = 12500, 212500, 96, 8
HD = D // HEADS
NT = -(-NODES // P)
ET = -(-EDGES // P)
LAST_ROWS = NODES - (NT - 1) * P
G = 4
RING = 4
BODY = G * RING
TURNS = -(-(ET + NT - 1) // BODY)
SCOLS = -(-((TURNS + 1) * BODY) // P)
STEPS = SCOLS * P
W0 = 2 * D
W1 = D + HEADS
PAIRS = NT // 2
BLOCKS = 7
BT = NT // BLOCKS
EPS_MSG, EPS_LN, EPS_Z, CLIP = 1e-7, 1e-5, 1e-6, 5.0


def build(nc, x, ids, dst_last, edge_t, w0, wqkv, we, out):
    ctx = ExitStack()
    with ctx:
        def sb(name, shape, dt=FP32):
            return ctx.enter_context(nc.sbuf_tensor(name, shape, dt))

        def ps(name, shape, dt=FP32):
            return ctx.enter_context(nc.psum_tensor(name, shape, dt))

        def sem(name):
            return ctx.enter_context(nc.semaphore(name))

        table0 = nc.dram_tensor("table0", (NT * P, W0), FP32, kind="Internal").ap()
        table1 = nc.dram_tensor("table1", (NT * P, 2 * D), FP32, kind="Internal").ap()
        steps_dram = nc.dram_tensor("steps_dram", (4, STEPS), I32, kind="Internal").ap()

        xs = sb("xs", [P, NT, D])
        sums = sb("sums", [P, NT * W0])
        qs = sb("qs", [P, NT * D])
        rows = sb("rows", [P, RING, G, W0])
        onehot = sb("onehot", [P, RING, G, P])
        score = sb("score", [P, G, HEADS])
        idx = sb("idx", [P, RING, G], I32)
        src_t = sb("src_t", [P, STEPS], U16)
        rel_t = sb("rel_t", [P, STEPS], BF16)
        step_tab = sb("step_tab", [4, STEPS], I32)
        iota_n = sb("iota_n", [P, P])
        ident = sb("ident", [P, P])
        w0_sb = sb("w0_sb", [D + 1, D])
        wqkv_sb = sb("wqkv_sb", [D + 1, 3 * D])
        we_sb = sb("we_sb", [D + 1, D])
        xt = sb("xt", [D + 1, 2, P])
        stage = sb("stage", [P, 2, D])
        stat = sb("stat", [P, 2, NT])
        gmax = sb("gmax", [P, 2])

        used = [0]

        def carve(home, shape, dt=FP32, parts=P):
            n = 1
            for c in shape:
                n *= c
            t = home[0:parts, used[0]:used[0] + n]
            used[0] += n
            if dt != FP32:
                t = t.bitcast(dt)
            if len(shape) == 2:
                t = t.rearrange("p (a b) -> p a b", b=shape[1])
            if len(shape) == 3:
                t = t.rearrange("p (a b c) -> p a b c", b=shape[1], c=shape[2])
            return t

        ids_g = carve(qs, [SCOLS, 2 * P], I32)
        rel_s = carve(qs, [SCOLS, P])
        src_s = carve(qs, [SCOLS, P])
        hit = carve(qs, [ET])
        small = carve(qs, [5, SCOLS])
        pack = carve(qs, [4, SCOLS])
        pack_i = carve(qs, [P], I32, 4 * SCOLS)
        step_i = carve(qs, [SCOLS], I32)
        iota_p = carve(qs, [P], I32)
        iota_s = carve(qs, [SCOLS], I32)
        assert used[0] <= NT * D
        last_i = rows[:, :, :, :].rearrange("p a b c -> p (a b c)")[:, 0:ET].bitcast(I32)
        end_step = onehot[:, :, :, :].rearrange("p a b c -> p (a b c)")[:, 0:ET]
        used[0] = NT * W1
        ea = carve(sums, [RING, G, P], parts=D + 1)
        onehot_t = carve(sums, [2, G, P])
        vals = carve(sums, [2, G, W1])
        prod = carve(sums, [G, D])
        iota_e = carve(sums, [ET], I32)
        assert used[0] <= NT * W0

        sums0 = sums[:, :].rearrange("p (k c) -> p k c", c=W0)
        sums1 = sums[:, 0:NT * W1].rearrange("p (k c) -> p k c", c=W1)
        kv_ring = rows[:, :, 0:2, :]
        sq = sums0[:, :, 0:D]
        sq1 = qs[:, :].rearrange("p (k c) -> p k c", c=D)

        feat = sq1

        ps_a = ps("ps_a", [P, 2, 2, 256])
        ps_a2 = ps("ps_a2", [P, 2, 2, 256])
        ps_sum0 = [ps_a, ps_a2]
        ps_t = ps("ps_t", [P, G, P])
        ps_x = [ps("ps_x0", [P, G, P]), ps("ps_x1", [P, G, P])]
        ps_misc = ps("ps_misc", [P, 4 * P])
        ps_e = [ps_a[:, 0].rearrange("p a b -> p (a b)")[:, 0:G * D], ps_a[:, 1].rearrange("p a b -> p (a b)")[:, 0:G * D]]
        ps_q = [ps_a2[:, 0].rearrange("p a b -> p (a b)")[:, 0:G * D], ps_a2[:, 1].rearrange("p a b -> p (a b)")[:, 0:G * D]]
        ps_sum1 = [ps_x[b][:, :, 0:W1] for b in range(2)]

        s_in = sem("s_in")
        s_x = sem("s_x")
        s_iota = sem("s_iota")
        s_dve = sem("s_dve")
        s_step = sem("s_step")
        s_ids = sem("s_ids")
        s_tin = sem("s_tin")
        s_tps = sem("s_tps")
        s_tcp = sem("s_tcp")
        s_pack = sem("s_pack")
        s_tab = sem("s_tab")
        s_gm = sem("s_gm")
        s_gall = sem("s_gall")
        s_gneg = sem("s_gneg")
        s_exp0 = sem("s_exp0")
        s_t0 = sem("s_t0")
        s_t0w = sem("s_t0w")
        s_slot = sem("s_slot")
        s_rows = [sem(f"s_rows{r}") for r in range(RING)]
        s_hot = sem("s_hot")
        s_sum = sem("s_sum")
        s_feat = sem("s_feat")
        s_xps = sem("s_xps")
        s_xt = sem("s_xt")
        s_h = sem("s_h")
        s_res = sem("s_res")
        s_cent = sem("s_cent")
        s_sq = sem("s_sq")
        s_var = sem("s_var")
        s_std = sem("s_std")
        s_x1 = sem("s_x1")
        s_fst = sem("s_fst")
        s_yst = sem("s_yst")
        s_yps = sem("s_yps")
        s_yt = sem("s_yt")
        s_qkv = sem("s_qkv")
        s_qcp = sem("s_qcp")
        s_kvcp = sem("s_kvcp")
        s_kvw = [sem(f"s_kvw{r}") for r in range(2)]
        s_slot1 = sem("s_slot1")
        s_rows1 = [sem(f"s_rows1_{r}") for r in range(RING)]
        s_ea = [sem(f"s_ea{r}") for r in range(RING)]
        s_hot1 = sem("s_hot1")
        s_tr = sem("s_tr")
        s_ones = sem("s_ones")
        s_trc = sem("s_trc")
        s_eu = sem("s_eu")
        s_qe = sem("s_qe")
        s_add = sem("s_add")
        s_add1 = sem("s_add1")
        s_mid = sem("s_mid")
        s_clip = sem("s_clip")
        s_exp1 = sem("s_exp1")
        s_vals = sem("s_vals")
        s_sum1 = sem("s_sum1")
        s_cent1 = sem("s_cent1")
        s_sq1 = sem("s_sq1")
        s_var1 = sem("s_var1")
        s_std1 = sem("s_std1")
        s_y = sem("s_y")
        s_out = sem("s_out")

        nodes = "(k p) c -> p k c"
        why = "the step table is clamped to the tiles when it is made"

        def step_values(engine, row, at, top):
            return nc.values_load_multi_w_load_instructions(
                step_tab[row:row + 1, bass.ds(at, G)], engines=[engine], min_val=0, max_val=top,
                skip_runtime_bounds_check_because=why)[1]

        block = ctx.enter_context(nc.Block())

        @block.sync
        def _(sp):
            sp.dma_start(last_i, dst_last.to_broadcast([P, ET])).then_inc(s_in, 16)
            sp.dma_start(xs[:, :, :], x.rearrange(nodes, p=P)).then_inc(s_x, 16)
            sp.dma_start(w0_sb[:, :], w0).then_inc(s_in, 16)
            sp.dma_start(wqkv_sb[:, :], wqkv).then_inc(s_in, 16)
            sp.dma_start(we_sb[:, :], we).then_inc(s_in, 16)
            sp.wait_ge(s_pack, 1)
            sp.dma_start(steps_dram.rearrange("q (j s) -> (q j) s", s=P), pack_i).then_inc(s_tab, 16)
            sp.wait_ge(s_tab, 16)
            sp.dma_start(step_tab[:, :], steps_dram).then_inc(s_tab, 16)
            for b in range(BLOCKS):
                sp.wait_ge(s_t0, b + 1)
                sp.dma_start(table0[b * BT * P:(b + 1) * BT * P].rearrange(nodes, p=P),
                             sums0[:, b * BT:(b + 1) * BT]).then_inc(s_t0w, 16)
            sp.wait_ge(s_kvcp, 1)
            sp.dma_start(table1[0:2 * P].rearrange(nodes, p=P), kv_ring[:, 0]).then_inc(s_kvw[0], 16)
            with sp.Fori(0, (PAIRS - 1) // 2) as i:
                for b in range(2):
                    sp.wait_ge(s_kvcp, i * 2 + (2 + b))
                    sp.dma_start(table1[bass.ds(i * (4 * P) + (2 + 2 * b) * P, 2 * P)].rearrange(nodes, p=P),
                                 kv_ring[:, (1 + b) % 2]).then_inc(s_kvw[(1 + b) % 2], 16)
            def load_edges(at, r):
                for u, tile in enumerate(step_values(SP_ENGINE, 3, at, ET - 1)):
                    sp.dma_start(ea[0:D, r, u, :],
                                 edge_t[bass.ds(tile, 1)].rearrange("a c e -> (a c) e")).then_inc(s_ea[r], 16)
            sp.wait_ge(s_var, 1)
            for r in range(RING):
                load_edges(r * G, r)
            with sp.Fori(0, TURNS) as i:
                for r in range(RING):
                    sp.wait_ge(s_eu, i * RING + (r + 1))
                    load_edges(i * BODY + (BODY + r * G), r)
            for b in range(BLOCKS):
                sp.wait_ge(s_y, b + 1)
                full = BT if b < BLOCKS - 1 else BT - 1
                sp.dma_start(out[b * BT * P:(b * BT + full) * P].rearrange(nodes, p=P),
                             xs[:, b * BT:b * BT + full]).then_inc(s_out, 16)
            sp.dma_start(out[(NT - 1) * P:NODES], xs[0:LAST_ROWS, NT - 1]).then_inc(s_out, 16)
            sp.wait_ge(s_out, 16 * (BLOCKS + 1))
            for r in range(RING):
                sp.wait_ge(s_ea[r], 16 * G * (TURNS + 1))

        @block.gpsimd
        def _(pool):
            pool.iota(iota_e, pattern=[[1, ET]], base=0, channel_multiplier=0).then_inc(s_iota, 1)
            pool.iota(iota_p, pattern=[[1, P]], base=0, channel_multiplier=0).then_inc(s_iota, 1)
            pool.iota(iota_s, pattern=[[P, SCOLS]], base=0, channel_multiplier=1).then_inc(s_iota, 1)
            pool.wait_ge(s_iota, 3)
            pool.memset(xt[D:D + 1, :, :], 1.0).then_inc(s_iota, 1)
            pool.wait_ge(s_iota, 4)
            pool.memset(ident[:, :], 1.0).then_inc(s_iota, 1)
            pool.wait_ge(s_iota, 5)
            pool.affine_select(out=ident[:, :], in_=ident[:, :], compare_op=ALU.is_equal, fill=0.0,
                               base=0, pattern=[[-1, P]], channel_multiplier=1).then_inc(s_iota, 1)
            pool.wait_ge(s_step, 1)
            for j in range(SCOLS):
                pool.indirect_dma_start(out=ids_g[:, j, :], out_offset=None, in_=ids,
                                        in_offset=bass.IndirectOffsetOnAxis(ap=step_i[:, j:j + 1], axis=0)
                                        ).then_inc(s_ids, 16)
            pool.wait_ge(s_gm, 1)
            pool.partition_all_reduce(gmax[:, 1:2], gmax[:, 0:1], P, bass.bass_isa.ReduceOp.max).then_inc(s_gall, 1)
            pool.wait_ge(s_t0w, 16 * BLOCKS)
            with pool.Fori(0, TURNS) as i:
                for r in range(RING):
                    pool.wait_ge(s_slot, i * RING + (r + 1))
                    pool.nop(nofuse=True)
                    for u in range(G):
                        pool.indirect_dma_start(out=rows[:, r, u, :], out_offset=None, in_=table0,
                                                in_offset=bass.IndirectOffsetOnAxis(ap=idx[:, r, u:u + 1], axis=0)
                                                ).then_inc(s_rows[r], 16)
            def stage_features(t, s_ready, s_staged, s_used):
                pool.wait_ge(s_ready, 1)
                pool.tensor_copy(stage[:, :, :], t[:, 0:2, :]).then_inc(s_staged, 1)
                with pool.Fori(1, PAIRS) as i:
                    pool.wait_ge(s_used, i)
                    pool.nop(nofuse=True)
                    pool.tensor_copy(stage[:, :, :], t[:, bass.ds(i * 2, 2), :]).then_inc(s_staged, 1)
            stage_features(feat, s_feat, s_fst, s_xps)
            stage_features(xs, s_x1, s_yst, s_yps)
            pool.wait_ge(s_kvw[0], 16 * ((PAIRS + 1) // 2))
            pool.wait_ge(s_kvw[1], 16 * (PAIRS // 2))
            pool.wait_ge(s_sq, 1)
            pool.memset(ea[D:D + 1, :, :, :], 1.0).then_inc(s_ones, 1)
            with pool.Fori(0, TURNS) as i:
                for r in range(RING):
                    pool.wait_ge(s_slot1, i * RING + (r + 1))
                    pool.nop(nofuse=True)
                    for u in range(G):
                        pool.indirect_dma_start(out=rows[:, r, u, :], out_offset=None, in_=table1,
                                                in_offset=bass.IndirectOffsetOnAxis(ap=idx[:, r, u:u + 1], axis=0)
                                                ).then_inc(s_rows1[r], 16)

        @block.tensor
        def _(pe):
            pe.wait_ge(s_iota, 6)
            for c in range(2 * SCOLS // 4 + 1):
                if c < 2 * SCOLS // 4:
                    pe.wait_ge(s_tin, 1 + (4 * c >= SCOLS))
                    if c:
                        pe.wait_ge(s_tcp, c)
                    for u in range(4):
                        n = 4 * c + u
                        m = rel_s[:, n, :] if n < SCOLS else src_s[:, n - SCOLS, :]
                        last = nc.tensor.transpose(ps_misc[:, u * P:(u + 1) * P], m, ident[:, :])
                    last.then_inc(s_tps, 1)
                else:
                    pe.wait_ge(s_tcp, c)
                    nc.tensor.transpose(ps_misc[0:4 * SCOLS, 0:P], pack[:, :, :].rearrange("p q j -> p (q j)"),
                                        ident[:, :]).then_inc(s_tps, 1)

            with pe.Fori(0, TURNS) as i:
                for r in range(RING):
                    pe.wait_ge(s_hot, i * RING + (r + 1))
                    pe.wait_ge(s_rows[r], i * (16 * G) + 16 * G)
                    for u in range(G):
                        last = nc.tensor.matmul(ps_sum0[r % 2][:, u // 2, u % 2, 0:W0], onehot[:, r, u, :],
                                                rows[:, r, u, :], start=True, stop=True)
                    last.then_inc(s_sum, 1)

            pe.wait_ge(s_feat, 1)
            with pe.Fori(0, PAIRS) as i:
                pe.wait_ge(s_fst, i + 1)
                for u in range(2):
                    last = nc.tensor.transpose(ps_misc[0:D, u * P:(u + 1) * P], stage[:, u, :], ident[:, :])
                last.then_inc(s_xps, 1)
                pe.wait_ge(s_xt, i + 1)
                for u in range(2):
                    last = nc.tensor.matmul(ps_x[0][:, u, 0:D], xt[:, u, :], w0_sb[:, :], start=True, stop=True)
                last.then_inc(s_h, 1)
                pe.wait_ge(s_res, i + 1)

            pe.wait_ge(s_x1, 1)
            with pe.Fori(0, PAIRS) as i:
                pe.wait_ge(s_yst, i + 1)
                for u in range(2):
                    last = nc.tensor.transpose(ps_misc[0:D, u * P:(u + 1) * P], stage[:, u, :], ident[:, :])
                last.then_inc(s_yps, 1)
                pe.wait_ge(s_yt, i + 1)
                for u in range(2):
                    nc.tensor.matmul(ps_t[:, u, 0:D], xt[:, u, :], wqkv_sb[:, 0:D], start=True, stop=True)
                    last = nc.tensor.matmul(ps_x[u][:, 0:2, :].rearrange("p a b -> p (a b)")[:, 0:2 * D],
                                            xt[:, u, :], wqkv_sb[:, D:3 * D], start=True, stop=True)
                last.then_inc(s_qkv, 1)
                pe.wait_ge(s_qcp, i + 1)
                pe.wait_ge(s_kvcp, i + 1)

            def scores_ahead(at, r, n, turn):
                pe.wait_ge(s_hot1, n)
                for u in range(G):
                    last = nc.tensor.transpose(ps_t[:, u, :], onehot[:, r, u, :], ident[:, :])
                last.then_inc(s_tr, 1)
                pe.wait_ge(s_ea[r], turn)
                for u in range(G):
                    last = nc.tensor.matmul(ps_e[r % 2][:, u * D:(u + 1) * D], ea[:, r, u, :], we_sb[:, :],
                                            start=True, stop=True)
                last.then_inc(s_eu, 1)
                offs = step_values(PE_ENGINE, 2, at, (NT - 1) * D)
                pe.wait_ge(s_trc, n)
                for u in range(G):
                    last = nc.tensor.matmul(ps_q[r % 2][:, u * D:(u + 1) * D], onehot_t[:, r % 2, u, :],
                                            qs[:, bass.ds(offs[u], D)], start=True, stop=True)
                last.then_inc(s_qe, 1)

            def sum_values(r, n):
                pe.wait_ge(s_vals, n)
                for u in range(G):
                    last = nc.tensor.matmul(ps_sum1[r % 2][:, u, :], onehot[:, r, u, :], vals[:, r % 2, u, :],
                                            start=True, stop=True)
                last.then_inc(s_sum1, 1)

            pe.wait_ge(s_tab, 32)
            pe.wait_ge(s_ones, 1)
            scores_ahead(0, 0, 1, 16 * G)
            for r in range(RING):
                if r:
                    sum_values(r - 1, r)
                scores_ahead((r + 1) * G, (r + 1) % RING, r + 2, 16 * G * (1 + (r == RING - 1)))
            with pe.Fori(1, TURNS) as i:
                for r in range(RING):
                    sum_values((r - 1) % RING, i * RING + r)
                    scores_ahead(i * BODY + (r + 1) * G, (r + 1) % RING, i * RING + (r + 2),
                                 i * (16 * G) + 16 * G * (1 + (r == RING - 1)))
            sum_values(RING - 1, TURNS * RING)

        @block.scalar
        def _(act):
            act.wait_ge(s_gneg, 1)
            for b in range(BLOCKS):
                nc.scalar.activation(sums0[:, b * BT:(b + 1) * BT, 0:D], sums0[:, b * BT:(b + 1) * BT, D:W0],
                                     ACT.Exp, bias=gmax[:, 0:1]).then_inc(s_exp0, 1)
            with act.Fori(0, PAIRS) as i:
                act.wait_ge(s_xps, i + 1)
                nc.scalar.copy(xt[0:D, :, :].rearrange("p a b -> p (a b)"), ps_misc[0:D, 0:2 * P]).then_inc(s_xt, 1)
            act.wait_ge(s_cent, 1)
            nc.scalar.activation(sq, xs[:, :, :], ACT.Square).then_inc(s_sq, 1)
            act.wait_ge(s_var, 1)
            nc.scalar.activation(stat[:, 1, :], stat[:, 0, :], ACT.Sqrt).then_inc(s_std, 1)
            def keys_values(i, b):
                act.wait_ge(s_yps, i + 1)
                nc.scalar.copy(xt[0:D, :, :].rearrange("p a b -> p (a b)"), ps_misc[0:D, 0:2 * P]).then_inc(s_yt, 1)
                act.wait_ge(s_qkv, i + 1)
                for u in range(2):
                    last = nc.scalar.copy(kv_ring[:, b, u, :], ps_x[u][:, 0:2, :].rearrange("p a b -> p (a b)")[:, 0:2 * D])
                last.then_inc(s_kvcp, 1)
            keys_values(0, 0)
            keys_values(1, 1)
            def later(i, b, turn):
                act.wait_ge(s_kvw[b], turn)
                keys_values(i, b)
            with act.Fori(1, (PAIRS - 1) // 2) as i:
                for b in range(2):
                    later(i * 2 + b, b, i * 16)
            later(PAIRS - 1, 0, 16 * ((PAIRS - 1) // 2))

            def copy_onehot(b, n):
                act.wait_ge(s_tr, n)
                nc.scalar.copy(onehot_t[:, b, :, :], ps_t[:, :, :]).then_inc(s_trc, 1)

            copy_onehot(0, 1)
            with act.Fori(0, TURNS) as i:
                for r in range(RING):
                    copy_onehot((r + 1) % 2, i * RING + (r + 2))
                    act.wait_ge(s_clip, i * RING + (r + 1))
                    nc.scalar.activation(vals[:, r % 2, :, D:W1], score[:, :, :], ACT.Exp).then_inc(s_exp1, 1)
            act.wait_ge(s_cent1, 1)
            nc.scalar.activation(sq1, xs[:, :, :], ACT.Square).then_inc(s_sq1, 1)
            act.wait_ge(s_var1, 1)
            nc.scalar.activation(stat[:, 1, :], stat[:, 0, :], ACT.Sqrt).then_inc(s_std1, 1)

        @block.vector
        def _(dve):
            chain = [0]

            def link(ins):
                chain[0] += 1
                ins.then_inc(s_dve, 1)
                dve.wait_ge(s_dve, chain[0])

            V = nc.vector
            cnt, kf, pen, kc = small[:, 0, :], small[:, 1, :], small[:, 2, :], small[:, 3, :]
            stepf = small[:, 4, :]
            dve.wait_ge(s_in, 64)
            dve.wait_ge(s_iota, 6)
            link(V.tensor_scalar(last_i, last_i, 7, None, ALU.logical_shift_right))
            link(V.tensor_copy(end_step, iota_e))
            link(V.tensor_tensor(end_step, end_step, last_i, ALU.add))
            V.tensor_copy(iota_n[:, :], iota_p)
            link(V.tensor_copy(stepf, iota_s))
            for j in range(SCOLS):
                link(V.tensor_scalar(hit, end_step, stepf[:, j:j + 1], None, ALU.is_lt, ALU.add, accum_out=cnt[:, j:j + 1]))
            link(V.tensor_tensor(kf, stepf, cnt, ALU.subtract))
            link(V.tensor_scalar(pen, cnt, float(ET), 1.0e6, ALU.is_ge, ALU.mult))
            link(V.tensor_scalar(pack[:, 3, :], cnt, float(ET - 1), None, ALU.min))
            V.tensor_copy(step_i, pack[:, 3, :]).then_inc(s_step, 1)
            link(V.tensor_scalar(kc, kf, float(NT - 1), None, ALU.min))
            V.tensor_scalar(pack[:, 0, :], kc, float(W0), None, ALU.mult)
            V.tensor_scalar(pack[:, 1, :], kc, float(W1), None, ALU.mult)
            V.tensor_scalar(pack[:, 2, :], kc, float(D), None, ALU.mult)
            link(V.tensor_scalar(kf, kf, float(P), None, ALU.mult))
            link(V.tensor_tensor(kf, kf, pen, ALU.add))
            dve.wait_ge(s_x, 16)
            m = sums0[:, :, D:W0]
            link(V.tensor_scalar(m, xs[:, :, :], 0.0, EPS_MSG, ALU.max, ALU.add))
            V.tensor_reduce(gmax[:, 0:1], m, AX.XY, ALU.max).then_inc(s_gm, 1)
            dve.wait_ge(s_gall, 1)
            V.tensor_scalar(gmax[:, 0:1], gmax[:, 1:2], -1.0, None, ALU.mult).then_inc(s_gneg, 1)
            dve.wait_ge(s_ids, 16 * SCOLS)
            for j in range(SCOLS):
                last = V.tensor_scalar(rel_s[:, j, :], ids_g[:, j, P:2 * P], kf[:, j:j + 1], None, ALU.subtract)
            last.then_inc(s_tin, 1)
            V.tensor_copy(src_s, ids_g[:, :, 0:P]).then_inc(s_tin, 1)
            for c in range(2 * SCOLS // 4):
                dve.wait_ge(s_tps, c + 1)
                for half in range(2):
                    n = 4 * c + 2 * half
                    t = rel_t if n < SCOLS else src_t
                    at = (n if n < SCOLS else n - SCOLS) * P
                    last = V.tensor_copy(t[:, at:at + 2 * P], ps_misc[:, half * 2 * P:(half + 1) * 2 * P])
                last.then_inc(s_tcp, 1)
            dve.wait_ge(s_tps, 2 * SCOLS // 4 + 1)
            V.tensor_copy(pack_i, ps_misc[0:4 * SCOLS, 0:P]).then_inc(s_pack, 1)
            for b in range(BLOCKS):
                dve.wait_ge(s_exp0, b + 1)
                t = sums0[:, b * BT:(b + 1) * BT]
                V.tensor_tensor(t[:, :, D:W0], t[:, :, D:W0], t[:, :, 0:D], ALU.mult).then_inc(s_t0, 1)

            def fill_slot(at, r, s):
                V.tensor_copy(idx[:, r, :], src_t[:, bass.ds(at, G)] if not isinstance(at, int) else src_t[:, at:at + G]
                              ).then_inc(s, 1)

            def make_onehot(at, r, u, n, s):
                rel = rel_t[:, bass.ds(at, n)] if not isinstance(at, int) else rel_t[:, at:at + n]
                ins = V.tensor_tensor(onehot[:, r, u:u + n, :], iota_n[:, :].unsqueeze(1).to_broadcast([P, n, P]),
                                      rel.unsqueeze(2).to_broadcast([P, n, P]), ALU.is_equal)
                if s is not None:
                    ins.then_inc(s, 1)

            for r in range(RING):
                fill_slot(r * G, r, s_slot)
            for r in range(2):
                make_onehot(r * G, r, 0, G, s_hot)
            dve.wait_ge(s_t0w, 16 * BLOCKS)
            dve.wait_ge(s_tab, 32)
            V.memset(sums[:, :], 0.0).then_inc(s_add, 1)
            with dve.Fori(0, TURNS) as i:
                for r in range(RING):
                    offs = step_values(DVE_ENGINE, 0, i * BODY + r * G, (NT - 1) * W0)
                    dve.wait_ge(s_sum, i * RING + (r + 1))
                    fill_slot(i * BODY + (BODY + r * G), r, s_slot)
                    for u in range(G):
                        dve.wait_ge(s_add, i * BODY + (r * G + u + 1))
                        acc = sums[:, bass.ds(offs[u], W0)]
                        V.tensor_tensor(acc, acc, ps_sum0[r % 2][:, u // 2, u % 2, 0:W0], ALU.add).then_inc(s_add, 1)
                        make_onehot(i * BODY + ((r + 2) * G + u), (r + 2) % RING, u, 1, s_hot if u == G - 1 else None)
            dve.wait_ge(s_add, TURNS * BODY + 1)
            f = feat
            link(V.tensor_scalar(f, sums0[:, :, 0:D], 0.0, None, ALU.is_equal))
            link(V.tensor_tensor(f, f, sums0[:, :, 0:D], ALU.add))
            link(V.reciprocal(f, f))
            link(V.tensor_tensor(f, f, sums0[:, :, D:W0], ALU.mult))
            V.tensor_tensor(f, f, xs[:, :, :], ALU.add).then_inc(s_feat, 1)
            with dve.Fori(0, PAIRS) as i:
                dve.wait_ge(s_h, i + 1)
                xv = xs[:, bass.ds(i * 2, 2), :]
                V.tensor_tensor(xv, xv, ps_x[0][:, 0:2, 0:D], ALU.add).then_inc(s_res, 1)
            dve.wait_ge(s_res, PAIRS)

            def layer_norm(s_c, s_s, s_v, s_r, squares):
                link(V.tensor_reduce(stat[:, 0, :], xs[:, :, :], AX.X, ALU.add))
                link(V.tensor_scalar(stat[:, 0, :], stat[:, 0, :], 1.0 / D, None, ALU.mult))
                V.tensor_tensor(xs[:, :, :], xs[:, :, :], stat[:, 0, :].unsqueeze(2).to_broadcast([P, NT, D]),
                                ALU.subtract).then_inc(s_c, 1)
                dve.wait_ge(s_s, 1)
                link(V.tensor_reduce(stat[:, 0, :], squares, AX.X, ALU.add))
                V.tensor_scalar(stat[:, 0, :], stat[:, 0, :], 1.0 / D, EPS_LN, ALU.mult, ALU.add).then_inc(s_v, 1)
                dve.wait_ge(s_r, 1)
                link(V.reciprocal(stat[:, 1, :], stat[:, 1, :]))

            layer_norm(s_cent, s_sq, s_var, s_std, sq)
            V.tensor_tensor(xs[:, :, :], xs[:, :, :], stat[:, 1, :].unsqueeze(2).to_broadcast([P, NT, D]),
                            ALU.mult).then_inc(s_x1, 1)
            V.memset(sums[:, 0:NT * W1], 0.0).then_inc(s_add1, 1)
            with dve.Fori(0, PAIRS) as i:
                dve.wait_ge(s_qkv, i + 1)
                for u in range(2):
                    last = V.tensor_scalar(qs[:, bass.ds(i * (2 * D) + u * D, D)], ps_t[:, u, 0:D],
                                           float(HD) ** -0.5, None, ALU.mult)
                last.then_inc(s_qcp, 1)

            def add_sums(at, r, n, done):
                offs = step_values(DVE_ENGINE, 1, at, (NT - 1) * W1)

                def add(u):
                    if u == 0:
                        dve.wait_ge(s_sum1, n)
                    dve.wait_ge(s_add1, done + (u + 1))
                    acc = sums[:, bass.ds(offs[u], W1)]
                    V.tensor_tensor(acc, acc, ps_sum1[r % 2][:, u, :], ALU.add).then_inc(s_add1, 1)
                return add

            def group(at, r, n, turn, before, mid):
                add = before or (lambda u: None)
                dve.wait_ge(s_rows1[r], turn)
                dve.wait_ge(s_qe, n)
                V.tensor_tensor(prod[:, :, :], rows[:, r, :, 0:D], ps_q[r % 2].rearrange("p (a b) -> p a b", b=D),
                                ALU.mult).then_inc(s_mid, 1)
                add(0)
                dve.wait_ge(s_mid, mid + 1)
                V.tensor_tensor(prod[:, :, :], prod[:, :, :], ps_e[r % 2].rearrange("p (a b) -> p a b", b=D),
                                ALU.mult).then_inc(s_mid, 1)
                add(1)
                dve.wait_ge(s_mid, mid + 2)
                V.tensor_reduce(score[:, :, :], prod[:, :, :].rearrange("p a (h d) -> p (a h) d", d=HD), AX.X,
                                ALU.add).then_inc(s_mid, 1)
                add(2)
                dve.wait_ge(s_mid, mid + 3)
                V.tensor_scalar(score[:, :, :], score[:, :, :], -CLIP, CLIP, ALU.max, ALU.min).then_inc(s_clip, 1)
                add(3)
                make_onehot(at + 2 * G, (r + 2) % RING, 0, G, s_hot1)
                dve.wait_ge(s_exp1, n)
                V.tensor_tensor(vals[:, r % 2, :, 0:D].rearrange("p a (h d) -> p a h d", d=HD),
                                rows[:, r, :, D:2 * D].rearrange("p a (h d) -> p a h d", d=HD),
                                vals[:, r % 2, :, D:W1].unsqueeze(3).to_broadcast([P, G, HEADS, HD]),
                                ALU.mult).then_inc(s_vals, 1)
                fill_slot(at + BODY, r, s_slot1)

            for r in range(RING):
                fill_slot(r * G, r, s_slot1)
            for r in range(2):
                make_onehot(r * G, r, 0, G, s_hot1)
            for r in range(RING):
                group(r * G, r, r + 1, 16 * G, add_sums((r - 1) * G, r - 1, r, (r - 1) * G) if r else None, 3 * r)
            with dve.Fori(1, TURNS) as i:
                for r in range(RING):
                    group(i * BODY + r * G, r, i * RING + (r + 1), i * (16 * G) + 16 * G,
                          add_sums(i * BODY + (r - 1) * G, (r - 1) % RING, i * RING + r, i * BODY + (r - 1) * G),
                          i * (3 * RING) + 3 * r)
            add = add_sums(TURNS * BODY - G, RING - 1, TURNS * RING, TURNS * BODY - G)
            for u in range(G):
                add(u)
            dve.wait_ge(s_add1, TURNS * BODY + 1)
            z = sums1[:, :, D:W1]
            link(V.tensor_scalar(z, z, EPS_Z, None, ALU.add))
            link(V.reciprocal(z, z))
            for h in range(HEADS):
                w = sums1[:, :, h * HD:(h + 1) * HD]
                last = V.tensor_tensor(w, w, z[:, :, h:h + 1].to_broadcast([P, NT, HD]), ALU.mult)
            link(last)
            link(V.tensor_tensor(xs[:, :, :], xs[:, :, :], sums1[:, :, 0:D], ALU.add))
            layer_norm(s_cent1, s_sq1, s_var1, s_std1, sq1)
            for b in range(BLOCKS):
                t = xs[:, b * BT:(b + 1) * BT]
                V.tensor_tensor(t, t, stat[:, 1, b * BT:(b + 1) * BT].unsqueeze(2).to_broadcast([P, BT, D]),
                                ALU.mult).then_inc(s_y, 1)


def kernel(x, src, dst, edge_attr_96, L0_gnn_W, L0_gnn_b, L1_gnn_Wq, L1_gnn_bq, L1_gnn_Wk, L1_gnn_bk,
           L1_gnn_We, L1_gnn_be, L1_gnn_Wv, L1_gnn_bv):
    import numpy as np
    import concourse.bacc as bacc
    from concourse.bass_utils import run_bass_kernel_spmd

    x, src, dst, edge, w0, b0, wq, bq, wk, bk, we, be, wv, bv = (
        np.asarray(a) for a in (x, src, dst, edge_attr_96, L0_gnn_W, L0_gnn_b, L1_gnn_Wq, L1_gnn_bq, L1_gnn_Wk,
                                L1_gnn_bk, L1_gnn_We, L1_gnn_be, L1_gnn_Wv, L1_gnn_bv))
    x_pad = np.concatenate([x, np.zeros((NT * P - NODES, D), x.dtype)])
    src = np.concatenate([src, np.zeros(ET * P - EDGES, src.dtype)]).reshape(ET, P)
    dst = np.concatenate([dst, np.full(ET * P - EDGES, NT * P - 1, dst.dtype)]).reshape(ET, P)
    edge = np.concatenate([edge, np.zeros((ET * P - EDGES, D), edge.dtype)])
    arrays = {
        "in_x": x_pad,
        "in_ids": np.concatenate([src, dst], axis=1),
        "in_dst_last": dst[:, P - 1].reshape(1, ET),
        "in_edge_t": edge.reshape(ET, P, D).transpose(0, 2, 1),
        "in_w0": np.concatenate([w0, b0[None]]),
        "in_wqkv": np.concatenate([np.concatenate([wq, wk, wv], axis=1), np.concatenate([bq, bk, bv])[None]]),
        "in_we": np.concatenate([we, be[None]]),
    }
    arrays = {k: np.ascontiguousarray(v) for k, v in arrays.items()}
    nc = bacc.Bacc("TRN2", target_bir_lowering=False, num_devices=1)
    aps = [nc.dram_tensor(k, v.shape, mybir.dt.from_np(v.dtype), kind="ExternalInput").ap()
           for k, v in arrays.items()]
    out = nc.dram_tensor("out", (NODES, D), FP32, kind="ExternalOutput").ap()
    build(nc, *aps, out)
    return run_bass_kernel_spmd(nc, [arrays], core_ids=[0]).results[0]["out"]
```

```python
from contextlib import ExitStack

import concourse.bass as bass
from concourse import mybir
from concourse.alu_op_type import AluOpType as ALU

FP32 = mybir.dt.float32
I32 = mybir.dt.int32
U16 = mybir.dt.uint16
BF16 = mybir.dt.bfloat16
ACT = mybir.ActivationFunctionType
AX = mybir.AxisListType
DVE_ENGINE = mybir.EngineType.DVE
PE_ENGINE = mybir.EngineType.PE
SP_ENGINE = mybir.EngineType.SP

P = 128
NODES, EDGES, D, HEADS = 12500, 212500, 96, 8
HD = D // HEADS
NT = -(-NODES // P)
ET = -(-EDGES // P)
LAST_ROWS = NODES - (NT - 1) * P
G = 4
RING = 4
BODY = G * RING
TURNS = -(-(ET + NT - 1) // BODY)
SCOLS = -(-((TURNS + 1) * BODY) // P)
STEPS = SCOLS * P
W0 = 2 * D
W1 = D + HEADS
C = 7
CHUNKS = NT // C
BLOCKS = 7
BT = NT // BLOCKS
TINY = 1e-37
EPS_MSG, EPS_LN, EPS_Z, CLIP = 1e-7, 1e-5, 1e-6, 5.0


def build(nc, x, ids, dst_last, edge_t, w0, wqkv, we, out):
    ctx = ExitStack()
    with ctx:
        def sb(name, shape, dt=FP32):
            return ctx.enter_context(nc.sbuf_tensor(name, shape, dt))

        def ps(name, shape, dt=FP32):
            return ctx.enter_context(nc.psum_tensor(name, shape, dt))

        def sem(name):
            return ctx.enter_context(nc.semaphore(name))

        table0 = nc.dram_tensor("table0", (NT * P, W0), FP32, kind="Internal").ap()
        table1 = nc.dram_tensor("table1", (NT * P, 2 * D), FP32, kind="Internal").ap()
        steps_dram = nc.dram_tensor("steps_dram", (4, STEPS), I32, kind="Internal").ap()

        xs = sb("xs", [P, NT, D])
        sums = sb("sums", [P, NT * W0])
        qs = sb("qs", [P, NT * D])
        rows = sb("rows", [P, RING, G, W0])
        onehot = sb("onehot", [P, RING, G, P])
        score = sb("score", [P, G, HEADS])
        idx = sb("idx", [P, RING, G], I32)
        src_t = sb("src_t", [P, STEPS], U16)
        rel_t = sb("rel_t", [P, STEPS], BF16)
        step_tab = sb("step_tab", [4, STEPS], I32)
        iota_n = sb("iota_n", [P, P])
        ident = sb("ident", [P, P])
        w0_sb = sb("w0_sb", [D + 1, D])
        wqkv_sb = sb("wqkv_sb", [D + 1, 3 * D])
        we_sb = sb("we_sb", [D + 1, D])
        xt = sb("xt", [D + 1, 2, C * P])
        ys = sb("ys", [P, 2, C, D])
        feat1 = sb("feat1", [P, C * D])
        bn = sb("bn", [P, C, 6])
        mv = sb("mv", [P, C, 2])
        std = sb("std", [P, C])
        scale = sb("scale", [P, 2, C, 2])
        zr = sb("zr", [P, 2, C, HEADS])
        xmax = sb("xmax", [P, BLOCKS])
        gmax = sb("gmax", [P, 3])

        used = [0]

        def carve(home, shape, dt=FP32, parts=P):
            n = 1
            for c in shape:
                n *= c
            t = home[0:parts, used[0]:used[0] + n]
            used[0] += n
            if dt != FP32:
                t = t.bitcast(dt)
            if len(shape) == 2:
                t = t.rearrange("p (a b) -> p a b", b=shape[1])
            if len(shape) == 3:
                t = t.rearrange("p (a b c) -> p a b c", b=shape[1], c=shape[2])
            return t

        ids_g = carve(qs, [SCOLS, 2 * P], I32)
        rel_s = carve(qs, [SCOLS, P])
        src_s = carve(qs, [SCOLS, P])
        hit = carve(qs, [ET])
        iota_e = hit.bitcast(I32)
        small = carve(qs, [5, SCOLS])
        pack = carve(qs, [4, SCOLS])
        pack_i = carve(qs, [P], I32, 4 * SCOLS)
        step_i = carve(qs, [SCOLS], I32)
        iota_p = carve(qs, [P], I32)
        iota_s = carve(qs, [SCOLS], I32)
        assert used[0] <= NT * D
        last_i = rows[:, :, :, :].rearrange("p a b c -> p (a b c)")[:, 0:ET].bitcast(I32)
        end_step = onehot[:, :, :, :].rearrange("p a b c -> p (a b c)")[:, 0:ET]
        used[0] = NT * W1
        ea = carve(sums, [RING, G, P], parts=D + 1)
        onehot_t = carve(sums, [2, G, P])
        vals = carve(sums, [2, G, W1])
        prod = carve(sums, [G, D])
        assert used[0] <= NT * W0

        sums0 = sums[:, :].rearrange("p (k c) -> p k c", c=W0)
        sums1 = sums[:, 0:NT * W1].rearrange("p (k c) -> p k c", c=W1)
        rows_flat = rows[:, :, :, :].rearrange("p a b c -> p (a b c)")
        onehot_flat = onehot[:, :, :, :].rearrange("p a b c -> p (a b c)")
        qkv = [t[:, 0:C * 3 * D].rearrange("p (k c) -> p k c", c=3 * D) for t in (rows_flat, onehot_flat)]
        feat = [t.rearrange("p (k c) -> p k c", c=D)
                for t in (rows_flat[:, C * 3 * D:C * 4 * D], feat1[:, :])]
        quot, done = ([rows_flat[:, (2 * a + b) * C * D:(2 * a + b + 1) * C * D].rearrange("p (k c) -> p k c", c=D)
                       for b in range(2)] for a in range(2))

        banks = ps("banks", [P, 8, 512])
        flat = banks[:, :, :].rearrange("p a b -> p (a b)")
        ps_sum0 = [banks[:, 2 * b:2 * b + 2, :].rearrange("p a (c d) -> p a c d", d=256) for b in range(2)]
        ps_tr = flat[0:D, 0:C * P]
        ps_h = banks[:, 2:4, :]
        ps_qkv = [banks[:, 4 + u % 4, 0:3 * D] for u in range(C)]
        ps_e = [banks[:, b, 0:G * D] for b in range(2)]
        ps_q = [banks[:, 2 + b, 0:G * D] for b in range(2)]
        ps_t = banks[:, 4, :].rearrange("p (a b) -> p a b", b=P)
        ps_sum1 = [banks[:, 5 + b, 0:G * W1].rearrange("p (a b) -> p a b", b=W1) for b in range(2)]
        ps_misc = banks[:, 7, :]

        s_last = sem("s_last")
        s_x = [sem(f"s_xin{b}") for b in range(BLOCKS)]
        s_w = sem("s_w")
        s_iota = sem("s_iota")
        s_wq = sem("s_wq")
        s_dve = sem("s_dve")
        s_step = sem("s_step")
        s_ids = sem("s_ids")
        s_tin = sem("s_tin")
        s_tps = sem("s_tps")
        s_tcp = sem("s_tcp")
        s_pack = sem("s_pack")
        s_tab = sem("s_tab")
        s_gm = sem("s_gm")
        s_gall = sem("s_gall")
        s_gneg = sem("s_gneg")
        s_relu = sem("s_relu")
        s_exp0 = sem("s_exp0")
        s_t0 = sem("s_t0")
        s_t0w = [sem(f"s_t0w{b}") for b in range(BLOCKS)]
        s_slot = sem("s_slot")
        s_rows = [sem(f"s_rows{r}") for r in range(RING)]
        s_hot = sem("s_hot")
        s_sum = sem("s_sum")
        s_add = sem("s_add")
        s_fch = sem("s_fch")
        s_feat = sem("s_feat")
        s_ftr = sem("s_ftr")
        s_ft = sem("s_ft")
        s_h = sem("s_h")
        s_y = sem("s_y")
        s_bn = sem("s_bn")
        s_ag = sem("s_ag")
        s_var = sem("s_var")
        s_std = sem("s_std")
        s_rec = sem("s_rec")
        s_scale = sem("s_scale")
        s_x1 = sem("s_x1")
        s_xcp = sem("s_xcp")
        s_ytr = sem("s_ytr")
        s_yt = sem("s_yt")
        s_qkv = sem("s_qkv")
        s_qcp = sem("s_qcp")
        s_ev = sem("s_ev")
        s_kvw = [sem(f"s_kvw{r}") for r in range(2)]
        s_zero = sem("s_zero")
        s_ones = sem("s_ones")
        s_slot1 = sem("s_slot1")
        s_rows1 = [sem(f"s_rows1_{r}") for r in range(RING)]
        s_ea = [sem(f"s_ea{r}") for r in range(RING)]
        s_hot1 = sem("s_hot1")
        s_tr = sem("s_tr")
        s_trc = sem("s_trc")
        s_eu = sem("s_eu")
        s_qe = sem("s_qe")
        s_mid = sem("s_mid")
        s_clip = sem("s_clip")
        s_exp1 = sem("s_exp1")
        s_vals = sem("s_vals")
        s_sum1 = sem("s_sum1")
        s_add1 = sem("s_add1")
        s_zch = sem("s_zch")
        s_out1 = sem("s_out1")
        s_y1 = sem("s_y1")
        s_bn1 = sem("s_bn1")
        s_ag1 = sem("s_ag1")
        s_var1 = sem("s_var1")
        s_std1 = sem("s_std1")
        s_rec1 = sem("s_rec1")
        s_scale1 = sem("s_scale1")
        s_y2 = sem("s_y2")
        s_out = [sem(f"s_stored{b}") for b in range(2)]

        nodes = "(k p) c -> p k c"
        why = "the step table is clamped to the tiles when it is made"

        def step_values(engine, row, at, top):
            return nc.values_load_multi_w_load_instructions(
                step_tab[row:row + 1, bass.ds(at, G)], engines=[engine], min_val=0, max_val=top,
                skip_runtime_bounds_check_because=why)[1]

        qs_tiles = qs[:, :].rearrange("p (k c) -> p k c", c=D)

        def tiles(t, k, n):
            return t[:, k:k + n, :] if isinstance(k, int) else t[:, bass.ds(k, n), :]

        def chunk_loop(engine, part):
            for c in range(4):
                part(c, c % 2, c // 2, True, c >= 1, c >= 2)
            with engine.Fori(0, (CHUNKS - 4) // 2) as i:
                for b in range(2):
                    part(i * 2 + (4 + b), b, i + 2, True, True, True)
            part(CHUNKS, 0, CHUNKS // 2, False, True, True)
            part(CHUNKS + 1, 1, CHUNKS // 2, False, False, True)

        block = ctx.enter_context(nc.Block())

        @block.sync
        def _(sp):
            sp.dma_start(last_i, dst_last.to_broadcast([P, ET])).then_inc(s_last, 16)
            for b in range(BLOCKS):
                sp.dma_start(xs[:, b * BT:(b + 1) * BT, :],
                             x[b * BT * P:(b + 1) * BT * P].rearrange(nodes, p=P)).then_inc(s_x[b], 16)
            sp.dma_start(w0_sb[:, :], w0).then_inc(s_w, 16)
            sp.dma_start(wqkv_sb[:, :], wqkv).then_inc(s_w, 16)
            sp.dma_start(we_sb[:, :], we).then_inc(s_w, 16)
            for b in range(BLOCKS):
                sp.wait_ge(s_t0, b + 1)
                sp.dma_start(table0[b * BT * P:(b + 1) * BT * P].rearrange(nodes, p=P),
                             sums0[:, b * BT:(b + 1) * BT]).then_inc(s_t0w[b], 16)
            sp.wait_ge(s_pack, 1)
            sp.dma_start(steps_dram.rearrange("q (j s) -> (q j) s", s=P), pack_i).then_inc(s_tab, 16)
            sp.wait_ge(s_tab, 16)
            sp.dma_start(step_tab[:, :], steps_dram).then_inc(s_tab, 16)
            with sp.Fori(0, CHUNKS // 2) as i:
                for b in range(2):
                    sp.wait_ge(s_ev, i * (2 * C) + (b + 1) * C)
                    sp.dma_start(table1[bass.ds(i * (2 * C * P) + b * C * P, C * P)].rearrange(nodes, p=P),
                                 qkv[b][:, :, D:3 * D]).then_inc(s_kvw[b], 16)
            def load_edges(at, r):
                for u, tile in enumerate(step_values(SP_ENGINE, 3, at, ET - 1)):
                    sp.dma_start(ea[0:D, r, u, :],
                                 edge_t[bass.ds(tile, 1)].rearrange("a c e -> (a c) e")).then_inc(s_ea[r], 16)
            sp.wait_ge(s_ones, 1)
            for r in range(RING):
                load_edges(r * G, r)
            with sp.Fori(0, TURNS) as i:
                for r in range(RING):
                    sp.wait_ge(s_eu, i * RING + (r + 1))
                    load_edges(i * BODY + (BODY + r * G), r)
            for r in range(RING):
                sp.wait_ge(s_ea[r], 16 * G * (TURNS + 1))
            with sp.Fori(0, CHUNKS // 2 - 1) as i:
                for b in range(2):
                    sp.wait_ge(s_y2, i * 2 + (b + 1))
                    sp.dma_start(out[bass.ds(i * (2 * C * P) + b * C * P, C * P)].rearrange(nodes, p=P),
                                 done[b]).then_inc(s_out[b], 16)
            at = (CHUNKS - 2) * C * P
            sp.wait_ge(s_y2, CHUNKS - 1)
            sp.dma_start(out[at:at + C * P].rearrange(nodes, p=P), done[0]).then_inc(s_out[0], 16)
            sp.wait_ge(s_y2, CHUNKS)
            sp.dma_start(out[at + C * P:(NT - 1) * P].rearrange(nodes, p=P), done[1][:, 0:C - 1]).then_inc(s_out[1], 16)
            sp.dma_start(out[(NT - 1) * P:NODES], done[1][0:LAST_ROWS, C - 1]).then_inc(s_out[1], 16)
            sp.wait_ge(s_out[0], 16 * CHUNKS // 2)
            sp.wait_ge(s_out[1], 16 * (CHUNKS // 2 + 1))

        @block.gpsimd
        def _(pool):
            pool.iota(iota_e, pattern=[[1, ET]], base=0, channel_multiplier=0).then_inc(s_iota, 1)
            pool.iota(iota_p, pattern=[[1, P]], base=0, channel_multiplier=0).then_inc(s_iota, 1)
            pool.iota(iota_s, pattern=[[P, SCOLS]], base=0, channel_multiplier=1).then_inc(s_iota, 1)
            pool.wait_ge(s_iota, 3)
            pool.memset(xt[D:D + 1, :, :], 1.0).then_inc(s_iota, 1)
            pool.wait_ge(s_iota, 4)
            pool.memset(ident[:, :], 1.0).then_inc(s_iota, 1)
            pool.wait_ge(s_iota, 5)
            pool.affine_select(out=ident[:, :], in_=ident[:, :], compare_op=ALU.is_equal, fill=0.0,
                               base=0, pattern=[[-1, P]], channel_multiplier=1).then_inc(s_iota, 1)
            pool.wait_ge(s_gm, 1)
            pool.partition_all_reduce(gmax[:, 1:2], gmax[:, 0:1], P, bass.bass_isa.ReduceOp.max).then_inc(s_gall, 1)
            pool.wait_ge(s_step, 1)
            for j in range(SCOLS):
                pool.indirect_dma_start(out=ids_g[:, j, :], out_offset=None, in_=ids,
                                        in_offset=bass.IndirectOffsetOnAxis(ap=step_i[:, j:j + 1], axis=0)
                                        ).then_inc(s_ids, 16)
            for b in range(BLOCKS):
                pool.wait_ge(s_t0w[b], 16)
            with pool.Fori(0, TURNS) as i:
                for r in range(RING):
                    pool.wait_ge(s_slot, i * RING + (r + 1))
                    pool.nop(nofuse=True)
                    for u in range(G):
                        pool.indirect_dma_start(out=rows[:, r, u, :], out_offset=None, in_=table0,
                                                in_offset=bass.IndirectOffsetOnAxis(ap=idx[:, r, u:u + 1], axis=0)
                                                ).then_inc(s_rows[r], 16)
            def keep(c, b, half, enters, norms, leaves):
                if leaves:
                    pool.wait_ge(s_ev, (c - 1) * C)
                    pool.nop(nofuse=True)
                    pool.tensor_copy(tiles(qs_tiles, (c - 2) * C, C), qkv[b][:, :, 0:D]).then_inc(s_qcp, 1)
                if norms:
                    pool.wait_ge(s_x1, c)
                    pool.nop(nofuse=True)
                    pool.tensor_copy(tiles(xs, (c - 1) * C, C), ys[:, 1 - b]).then_inc(s_xcp, 1)
                if not enters and norms:
                    pool.memset(sums[:, 0:NT * W1], 0.0).then_inc(s_zero, 1)
                    pool.wait_ge(s_zero, 1)
                    pool.memset(ea[D:D + 1, :, :, :], 1.0).then_inc(s_ones, 1)
                    pool.wait_ge(s_ones, 1)
            chunk_loop(pool, keep)
            for b in range(2):
                pool.wait_ge(s_kvw[b], 16 * (CHUNKS // 2))
            with pool.Fori(0, TURNS) as i:
                for r in range(RING):
                    pool.wait_ge(s_slot1, i * RING + (r + 1))
                    pool.nop(nofuse=True)
                    for u in range(G):
                        pool.indirect_dma_start(out=rows[:, r, u, :], out_offset=None, in_=table1,
                                                in_offset=bass.IndirectOffsetOnAxis(ap=idx[:, r, u:u + 1], axis=0)
                                                ).then_inc(s_rows1[r], 16)

            def residual(c, b):
                pool.wait_ge(s_out1, c + 1)
                pool.nop(nofuse=True)
                if not isinstance(c, int):
                    pool.wait_ge(s_y2, c - 1)
                    pool.nop(nofuse=True)
                pool.tensor_tensor(ys[:, b], quot[b], tiles(xs, c * C, C), ALU.add).then_inc(s_y1, 1)
            for b in range(2):
                residual(b, b)
            with pool.Fori(1, CHUNKS // 2) as i:
                for b in range(2):
                    residual(i * 2 + b, b)

        @block.tensor
        def _(pe):
            pe.wait_ge(s_iota, 6)
            for c in range(2 * SCOLS // 4 + 1):
                if c < 2 * SCOLS // 4:
                    pe.wait_ge(s_tin, 1 + (4 * c >= SCOLS))
                    if c:
                        pe.wait_ge(s_tcp, c)
                    for u in range(4):
                        n = 4 * c + u
                        m = rel_s[:, n, :] if n < SCOLS else src_s[:, n - SCOLS, :]
                        last = nc.tensor.transpose(ps_misc[:, u * P:(u + 1) * P], m, ident[:, :])
                    last.then_inc(s_tps, 1)
                else:
                    pe.wait_ge(s_tcp, c)
                    nc.tensor.transpose(ps_misc[0:4 * SCOLS, 0:P], pack[:, :, :].rearrange("p q j -> p (q j)"),
                                        ident[:, :]).then_inc(s_tps, 1)

            with pe.Fori(0, TURNS) as i:
                for r in range(RING):
                    pe.wait_ge(s_hot, i * RING + (r + 1))
                    pe.wait_ge(s_rows[r], i * (16 * G) + 16 * G)
                    for u in range(G):
                        last = nc.tensor.matmul(ps_sum0[r % 2][:, u // 2, u % 2, 0:W0], onehot[:, r, u, :],
                                                rows[:, r, u, :], start=True, stop=True)
                    last.then_inc(s_sum, 1)

            def products(c, b, half, enters, norms, leaves):
                if leaves:
                    pe.wait_ge(s_x1, c - 1)
                    for u in range(C):
                        last = nc.tensor.transpose(ps_tr[:, u * P:(u + 1) * P], ys[:, b, u, :], ident[:, :])
                    last.then_inc(s_ytr, 1)
                    pe.wait_ge(s_yt, c - 1)
                    for u in range(C):
                        if u >= 4:
                            pe.wait_ge(s_ev, (c - 2) * C + (u - 3))
                        nc.tensor.matmul(ps_qkv[u], xt[:, 1, u * P:(u + 1) * P], wqkv_sb[:, :],
                                         start=True, stop=True).then_inc(s_qkv, 1)
                if enters:
                    pe.wait_ge(s_feat, c + 1)
                    for u in range(C):
                        last = nc.tensor.transpose(ps_tr[:, u * P:(u + 1) * P], feat[b][:, u, :], ident[:, :])
                    last.then_inc(s_ftr, 1)
                    pe.wait_ge(s_ft, c + 1)
                    if norms:
                        pe.wait_ge(s_y, c)
                    for u in range(C):
                        last = nc.tensor.matmul(ps_h[:, u // 4, (u % 4) * D:(u % 4 + 1) * D],
                                                xt[:, 0, u * P:(u + 1) * P], w0_sb[:, :], start=True, stop=True)
                    last.then_inc(s_h, 1)

            pe.wait_ge(s_wq, 1)
            chunk_loop(pe, products)

            def scores_ahead(at, r, n, turn):
                pe.wait_ge(s_hot1, n)
                for u in range(G):
                    last = nc.tensor.transpose(ps_t[:, u, :], onehot[:, r, u, :], ident[:, :])
                last.then_inc(s_tr, 1)
                pe.wait_ge(s_ea[r], turn)
                for u in range(G):
                    last = nc.tensor.matmul(ps_e[r % 2][:, u * D:(u + 1) * D], ea[:, r, u, :], we_sb[:, :],
                                            start=True, stop=True)
                last.then_inc(s_eu, 1)
                offs = step_values(PE_ENGINE, 2, at, (NT - 1) * D)
                pe.wait_ge(s_trc, n)
                for u in range(G):
                    last = nc.tensor.matmul(ps_q[r % 2][:, u * D:(u + 1) * D], onehot_t[:, r % 2, u, :],
                                            qs[:, bass.ds(offs[u], D)], start=True, stop=True)
                last.then_inc(s_qe, 1)

            def sum_values(r, n):
                pe.wait_ge(s_vals, n)
                for u in range(G):
                    last = nc.tensor.matmul(ps_sum1[r % 2][:, u, :], onehot[:, r, u, :], vals[:, r % 2, u, :],
                                            start=True, stop=True)
                last.then_inc(s_sum1, 1)

            pe.wait_ge(s_tab, 32)
            pe.wait_ge(s_ones, 1)
            pe.wait_ge(s_ev, NT)
            pe.wait_ge(s_qcp, CHUNKS)
            scores_ahead(0, 0, 1, 16 * G)
            for r in range(RING):
                if r:
                    sum_values(r - 1, r)
                scores_ahead((r + 1) * G, (r + 1) % RING, r + 2, 16 * G * (1 + (r == RING - 1)))
            with pe.Fori(1, TURNS) as i:
                for r in range(RING):
                    sum_values((r - 1) % RING, i * RING + r)
                    scores_ahead(i * BODY + (r + 1) * G, (r + 1) % RING, i * RING + (r + 2),
                                 i * (16 * G) + 16 * G * (1 + (r == RING - 1)))
            sum_values(RING - 1, TURNS * RING)

        @block.scalar
        def _(act):
            for b in range(BLOCKS):
                act.wait_ge(s_x[b], 16)
                nc.scalar.activation(sums0[:, b * BT:(b + 1) * BT, D:W0], xs[:, b * BT:(b + 1) * BT],
                                     ACT.Relu).then_inc(s_relu, 1)
            act.wait_ge(s_gneg, 1)
            for b in range(BLOCKS):
                act.wait_ge(s_relu, b + 1)
                nc.scalar.activation(sums0[:, b * BT:(b + 1) * BT, 0:D], sums0[:, b * BT:(b + 1) * BT, D:W0],
                                     ACT.Exp, bias=gmax[:, 2:3]).then_inc(s_exp0, 1)

            def chunk(c, b, half, enters, norms, leaves):
                if leaves:
                    act.wait_ge(s_ytr, c - 1)
                    nc.scalar.copy(xt[0:D, 1, :], ps_tr).then_inc(s_yt, 1)
                    if not isinstance(c, int) or c >= 4:
                        act.wait_ge(s_kvw[b], (half - 1) * 16)
                        act.wait_ge(s_qcp, c - 3)
                    for u in range(C):
                        act.wait_ge(s_qkv, (c - 2) * C + (u + 1))
                        nc.scalar.copy(qkv[b][:, u, :], ps_qkv[u]).then_inc(s_ev, 1)
                if enters:
                    act.wait_ge(s_ftr, c + 1)
                    nc.scalar.copy(xt[0:D, 0, :], ps_tr).then_inc(s_ft, 1)
                if norms:
                    act.wait_ge(s_var, c)
                    nc.scalar.activation(std[:, :], mv[:, :, 1], ACT.Sqrt).then_inc(s_std, 1)
                    act.wait_ge(s_scale, c)
                    for u in range(C):
                        y = ys[:, 1 - b, u, :]
                        last = nc.scalar.activation(y, y, ACT.Identity, bias=scale[:, 1 - b, u, 1:2],
                                                    scale=scale[:, 1 - b, u, 0:1])
                    last.then_inc(s_x1, 1)

            chunk_loop(act, chunk)

            def copy_onehot(b, n):
                act.wait_ge(s_tr, n)
                nc.scalar.copy(onehot_t[:, b, :, :], ps_t[:, :, :]).then_inc(s_trc, 1)

            copy_onehot(0, 1)
            with act.Fori(0, TURNS) as i:
                for r in range(RING):
                    copy_onehot((r + 1) % 2, i * RING + (r + 2))
                    act.wait_ge(s_clip, i * RING + (r + 1))
                    nc.scalar.activation(vals[:, r % 2, :, D:W1], score[:, :, :], ACT.Exp).then_inc(s_exp1, 1)
            def norm(c, b, half):
                act.wait_ge(s_var1, c + 1)
                nc.scalar.activation(std[:, :], mv[:, :, 1], ACT.Sqrt).then_inc(s_std1, 1)
                if half is not None:
                    act.wait_ge(s_out[b], half * 16)
                act.wait_ge(s_scale1, c + 1)
                for u in range(C):
                    last = nc.scalar.activation(done[b][:, u, :], ys[:, b, u, :], ACT.Identity,
                                                bias=scale[:, b, u, 1:2], scale=scale[:, b, u, 0:1])
                last.then_inc(s_y2, 1)
            for b in range(2):
                norm(b, b, None)
            with act.Fori(1, CHUNKS // 2) as i:
                for b in range(2):
                    norm(i * 2 + b, b, i)

        @block.vector
        def _(dve):
            chain = [0]

            def link(ins):
                chain[0] += 1
                ins.then_inc(s_dve, 1)
                dve.wait_ge(s_dve, chain[0])

            V = nc.vector
            cnt, kf, pen, kc = small[:, 0, :], small[:, 1, :], small[:, 2, :], small[:, 3, :]
            stepf = small[:, 4, :]
            dve.wait_ge(s_last, 16)
            dve.wait_ge(s_iota, 6)
            link(V.tensor_scalar(last_i, last_i, 7, None, ALU.logical_shift_right))
            link(V.tensor_copy(end_step, iota_e))
            link(V.tensor_tensor(end_step, end_step, last_i, ALU.add))
            V.tensor_copy(iota_n[:, :], iota_p)
            link(V.tensor_copy(stepf, iota_s))

            def count_ended(j):
                link(V.tensor_scalar(hit, end_step, stepf[:, j:j + 1], None, ALU.is_lt, ALU.add,
                                     accum_out=cnt[:, j:j + 1]))

            for j in range(4):
                count_ended(j)
            for b in range(BLOCKS):
                dve.wait_ge(s_x[b], 16)
                last = V.tensor_reduce(xmax[:, b:b + 1], xs[:, b * BT:(b + 1) * BT, :], AX.XY, ALU.max)
                if b == 3:
                    for j in range(4, 7):
                        count_ended(j)
            link(last)
            V.tensor_reduce(gmax[:, 0:1], xmax[:, :], AX.X, ALU.max).then_inc(s_gm, 1)
            for j in range(7, 10):
                count_ended(j)
            dve.wait_ge(s_gall, 1)
            V.tensor_scalar(gmax[:, 2:3], gmax[:, 1:2], 0.0, -1.0, ALU.max, ALU.mult).then_inc(s_gneg, 1)
            for j in range(10, SCOLS):
                count_ended(j)
            link(V.tensor_tensor(kf, stepf, cnt, ALU.subtract))
            link(V.tensor_scalar(pen, cnt, float(ET), 1.0e6, ALU.is_ge, ALU.mult))
            link(V.tensor_scalar(pack[:, 3, :], cnt, float(ET - 1), None, ALU.min))
            V.tensor_copy(step_i, pack[:, 3, :]).then_inc(s_step, 1)
            link(V.tensor_scalar(kc, kf, float(NT - 1), None, ALU.min))
            V.tensor_scalar(pack[:, 0, :], kc, float(W0), None, ALU.mult)
            V.tensor_scalar(pack[:, 1, :], kc, float(W1), None, ALU.mult)
            V.tensor_scalar(pack[:, 2, :], kc, float(D), None, ALU.mult)
            link(V.tensor_scalar(kf, kf, float(P), None, ALU.mult))
            link(V.tensor_tensor(kf, kf, pen, ALU.add))
            for b in range(BLOCKS):
                dve.wait_ge(s_exp0, b + 1)
                t = sums0[:, b * BT:(b + 1) * BT]
                V.scalar_tensor_tensor(out=t[:, :, D:W0], in0=t[:, :, D:W0], scalar=EPS_MSG, in1=t[:, :, 0:D],
                                       op0=ALU.add, op1=ALU.mult).then_inc(s_t0, 1)
            dve.wait_ge(s_ids, 16 * SCOLS)
            for j in range(SCOLS):
                last = V.tensor_scalar(rel_s[:, j, :], ids_g[:, j, P:2 * P], kf[:, j:j + 1], None, ALU.subtract)
            last.then_inc(s_tin, 1)
            V.tensor_copy(src_s, ids_g[:, :, 0:P]).then_inc(s_tin, 1)
            for c in range(2 * SCOLS // 4):
                dve.wait_ge(s_tps, c + 1)
                for half in range(2):
                    n = 4 * c + 2 * half
                    t = rel_t if n < SCOLS else src_t
                    at = (n if n < SCOLS else n - SCOLS) * P
                    last = V.tensor_copy(t[:, at:at + 2 * P], ps_misc[:, half * 2 * P:(half + 1) * 2 * P])
                last.then_inc(s_tcp, 1)
            dve.wait_ge(s_tps, 2 * SCOLS // 4 + 1)
            V.tensor_copy(pack_i, ps_misc[0:4 * SCOLS, 0:P]).then_inc(s_pack, 1)

            dve.wait_ge(s_w, 48)
            V.tensor_scalar(wqkv_sb[:, 0:D], wqkv_sb[:, 0:D], float(HD) ** -0.5, None, ALU.mult).then_inc(s_wq, 1)

            def fill_slot(at, r, s):
                V.tensor_copy(idx[:, r, :], src_t[:, bass.ds(at, G)] if not isinstance(at, int) else src_t[:, at:at + G]
                              ).then_inc(s, 1)

            def make_onehot(at, r, u, n, s):
                rel = rel_t[:, bass.ds(at, n)] if not isinstance(at, int) else rel_t[:, at:at + n]
                ins = V.tensor_tensor(onehot[:, r, u:u + n, :], iota_n[:, :].unsqueeze(1).to_broadcast([P, n, P]),
                                      rel.unsqueeze(2).to_broadcast([P, n, P]), ALU.is_equal)
                if s is not None:
                    ins.then_inc(s, 1)

            for r in range(RING):
                fill_slot(r * G, r, s_slot)
            for r in range(2):
                make_onehot(r * G, r, 0, G, s_hot)
            for b in range(BLOCKS):
                dve.wait_ge(s_t0w[b], 16)
                last = V.memset(sums0[:, b * BT:(b + 1) * BT], 0.0)
            last.then_inc(s_add, 1)
            dve.wait_ge(s_tab, 32)
            with dve.Fori(0, TURNS) as i:
                for r in range(RING):
                    offs = step_values(DVE_ENGINE, 0, i * BODY + r * G, (NT - 1) * W0)
                    dve.wait_ge(s_sum, i * RING + (r + 1))
                    fill_slot(i * BODY + (BODY + r * G), r, s_slot)
                    for u in range(G):
                        dve.wait_ge(s_add, i * BODY + (r * G + u + 1))
                        acc = sums[:, bass.ds(offs[u], W0)]
                        V.tensor_tensor(acc, acc, ps_sum0[r % 2][:, u // 2, u % 2, 0:W0], ALU.add).then_inc(s_add, 1)
                        make_onehot(i * BODY + ((r + 2) * G + u), (r + 2) % RING, u, 1, s_hot if u == G - 1 else None)
            dve.wait_ge(s_add, TURNS * BODY + 1)

            def statistics(b, c, s_in, s_bn, s_ag, s_var):
                def stats():
                    dve.wait_ge(s_in, c)
                    for u in range(C):
                        last = V.bn_stats(bn[:, u, :], ys[:, b, u, :])
                    last.then_inc(s_bn, 1)

                def aggregate():
                    dve.wait_ge(s_bn, c)
                    dve.nop(nofuse=True)
                    for u in range(C):
                        last = V.bn_aggr(mv[:, u, :], bn[:, u, :])
                    last.then_inc(s_ag, 1)

                def variance():
                    dve.wait_ge(s_ag, c)
                    V.tensor_scalar(mv[:, :, 1], mv[:, :, 1], EPS_LN, None, ALU.add).then_inc(s_var, 1)
                return stats, aggregate, variance

            def scales(b, c, s_std, s_rec, s_scale):
                dve.wait_ge(s_std, c)
                V.reciprocal(scale[:, b, :, 0], std[:, :]).then_inc(s_rec, 1)
                dve.wait_ge(s_rec, c)
                V.scalar_tensor_tensor(out=scale[:, b, :, 1], in0=mv[:, :, 0], scalar=-1.0, in1=scale[:, b, :, 0],
                                       op0=ALU.mult, op1=ALU.mult).then_inc(s_scale, 1)

            def nothing():
                pass

            def chunk(c, b, half, enters, norms, leaves):
                f = feat[b]
                if enters:
                    n = c * 3
                    t = tiles(sums0, c * C, C)
                    V.tensor_scalar(f, t[:, :, 0:D], TINY, None, ALU.max).then_inc(s_fch, 1)
                stats = aggregate = variance = nothing
                if norms:
                    dve.wait_ge(s_h, c)
                    if not isinstance(c, int) or c > 2:
                        dve.wait_ge(s_xcp, c - 2)
                        dve.wait_ge(s_ytr, c - 2)
                    for lo, hi in ((0, 4), (4, C)):
                        last = V.tensor_tensor(ys[:, 1 - b, lo:hi, :], tiles(xs, (c - 1) * C + lo, hi - lo),
                                               ps_h[:, lo // 4, 0:(hi - lo) * D].rearrange("p (a b) -> p a b", b=D),
                                               ALU.add)
                    last.then_inc(s_y, 1)
                    stats, aggregate, variance = statistics(1 - b, c, s_y, s_bn, s_ag, s_var)
                if enters:
                    dve.wait_ge(s_fch, n + 1)
                    V.reciprocal(f, f).then_inc(s_fch, 1)
                stats()
                if enters:
                    dve.wait_ge(s_fch, n + 2)
                    V.tensor_tensor(f, f, t[:, :, D:W0], ALU.mult).then_inc(s_fch, 1)
                aggregate()
                if enters:
                    dve.wait_ge(s_fch, n + 3)
                    V.tensor_tensor(f, f, tiles(xs, c * C, C), ALU.add).then_inc(s_feat, 1)
                variance()
                if norms:
                    scales(1 - b, c, s_std, s_rec, s_scale)

            chunk_loop(dve, chunk)
            V.memset(zr[:, :, :, :], 0.0).then_inc(s_add1, 1)
            dve.wait_ge(s_zero, 1)
            dve.wait_ge(s_kvw[1], 16 * (CHUNKS // 2))
            dve.wait_ge(s_qcp, CHUNKS)

            def add_sums(at, r, n, done):
                offs = step_values(DVE_ENGINE, 1, at, (NT - 1) * W1)

                def add(u):
                    if u == 0:
                        dve.wait_ge(s_sum1, n)
                    dve.wait_ge(s_add1, done + (u + 1))
                    acc = sums[:, bass.ds(offs[u], W1)]
                    V.tensor_tensor(acc, acc, ps_sum1[r % 2][:, u, :], ALU.add).then_inc(s_add1, 1)
                return add

            def group(at, r, n, turn, before, mid):
                add = before or (lambda u: None)
                dve.wait_ge(s_rows1[r], turn)
                dve.wait_ge(s_qe, n)
                V.tensor_tensor(prod[:, :, :], rows[:, r, :, 0:D], ps_q[r % 2].rearrange("p (a b) -> p a b", b=D),
                                ALU.mult).then_inc(s_mid, 1)
                add(0)
                dve.wait_ge(s_mid, mid + 1)
                V.tensor_tensor(prod[:, :, :], prod[:, :, :], ps_e[r % 2].rearrange("p (a b) -> p a b", b=D),
                                ALU.mult).then_inc(s_mid, 1)
                add(1)
                dve.wait_ge(s_mid, mid + 2)
                V.tensor_reduce(score[:, :, :], prod[:, :, :].rearrange("p a (h d) -> p (a h) d", d=HD), AX.X,
                                ALU.add).then_inc(s_mid, 1)
                add(2)
                dve.wait_ge(s_mid, mid + 3)
                V.tensor_scalar(score[:, :, :], score[:, :, :], -CLIP, CLIP, ALU.max, ALU.min).then_inc(s_clip, 1)
                add(3)
                make_onehot(at + 2 * G, (r + 2) % RING, 0, G, s_hot1)
                dve.wait_ge(s_exp1, n)
                V.tensor_tensor(vals[:, r % 2, :, 0:D].rearrange("p a (h d) -> p a h d", d=HD),
                                rows[:, r, :, D:2 * D].rearrange("p a (h d) -> p a h d", d=HD),
                                vals[:, r % 2, :, D:W1].unsqueeze(3).to_broadcast([P, G, HEADS, HD]),
                                ALU.mult).then_inc(s_vals, 1)
                fill_slot(at + BODY, r, s_slot1)

            for r in range(RING):
                fill_slot(r * G, r, s_slot1)
            for r in range(2):
                make_onehot(r * G, r, 0, G, s_hot1)
            for r in range(RING):
                group(r * G, r, r + 1, 16 * G, add_sums((r - 1) * G, r - 1, r, (r - 1) * G) if r else None, 3 * r)
            with dve.Fori(1, TURNS) as i:
                for r in range(RING):
                    group(i * BODY + r * G, r, i * RING + (r + 1), i * (16 * G) + 16 * G,
                          add_sums(i * BODY + (r - 1) * G, (r - 1) % RING, i * RING + r, i * BODY + (r - 1) * G),
                          i * (3 * RING) + 3 * r)
            add = add_sums(TURNS * BODY - G, RING - 1, TURNS * RING, TURNS * BODY - G)
            for u in range(G):
                add(u)
            dve.wait_ge(s_add1, TURNS * BODY + 1)

            def end_chunk(c, b, half, enters, norms, leaves):
                stats = aggregate = variance = nothing
                if norms:
                    stats, aggregate, variance = statistics(1 - b, c, s_y1, s_bn1, s_ag1, s_var1)
                if enters:
                    t = tiles(sums1, c * C, C)
                    n = c * 2
                    V.tensor_scalar(zr[:, b], t[:, :, D:W1], EPS_Z, None, ALU.add).then_inc(s_zch, 1)
                stats()
                if enters:
                    dve.wait_ge(s_zch, n + 1)
                    V.reciprocal(zr[:, b], zr[:, b]).then_inc(s_zch, 1)
                aggregate()
                if enters:
                    dve.wait_ge(s_zch, n + 2)
                    V.tensor_tensor(quot[b].rearrange("p k (h d) -> p k h d", d=HD),
                                    t[:, :, 0:D].rearrange("p k (h d) -> p k h d", d=HD),
                                    zr[:, b].unsqueeze(3).to_broadcast([P, C, HEADS, HD]), ALU.mult).then_inc(s_out1, 1)
                variance()
                if norms:
                    scales(1 - b, c, s_std1, s_rec1, s_scale1)
            chunk_loop(dve, end_chunk)


def kernel(x, src, dst, edge_attr_96, L0_gnn_W, L0_gnn_b, L1_gnn_Wq, L1_gnn_bq, L1_gnn_Wk, L1_gnn_bk,
           L1_gnn_We, L1_gnn_be, L1_gnn_Wv, L1_gnn_bv):
    import numpy as np
    import concourse.bacc as bacc
    from concourse.bass_utils import run_bass_kernel_spmd

    x, src, dst, edge, w0, b0, wq, bq, wk, bk, we, be, wv, bv = (
        np.asarray(a) for a in (x, src, dst, edge_attr_96, L0_gnn_W, L0_gnn_b, L1_gnn_Wq, L1_gnn_bq, L1_gnn_Wk,
                                L1_gnn_bk, L1_gnn_We, L1_gnn_be, L1_gnn_Wv, L1_gnn_bv))
    x_pad = np.concatenate([x, np.zeros((NT * P - NODES, D), x.dtype)])
    src = np.concatenate([src, np.zeros(ET * P - EDGES, src.dtype)]).reshape(ET, P)
    dst = np.concatenate([dst, np.full(ET * P - EDGES, NT * P - 1, dst.dtype)]).reshape(ET, P)
    edge = np.concatenate([edge, np.zeros((ET * P - EDGES, D), edge.dtype)])
    arrays = {
        "in_x": x_pad,
        "in_ids": np.concatenate([src, dst], axis=1),
        "in_dst_last": dst[:, P - 1].reshape(1, ET),
        "in_edge_t": edge.reshape(ET, P, D).transpose(0, 2, 1),
        "in_w0": np.concatenate([w0, b0[None]]),
        "in_wqkv": np.concatenate([np.concatenate([wq, wk, wv], axis=1), np.concatenate([bq, bk, bv])[None]]),
        "in_we": np.concatenate([we, be[None]]),
    }
    arrays = {k: np.ascontiguousarray(v) for k, v in arrays.items()}
    nc = bacc.Bacc("TRN2", target_bir_lowering=False, num_devices=1)
    aps = [nc.dram_tensor(k, v.shape, mybir.dt.from_np(v.dtype), kind="ExternalInput").ap()
           for k, v in arrays.items()]
    out = nc.dram_tensor("out", (NODES, D), FP32, kind="ExternalOutput").ap()
    build(nc, *aps, out)
    return run_bass_kernel_spmd(nc, [arrays], core_ids=[0]).results[0]["out"]
```

```python
from contextlib import ExitStack

import concourse.bass as bass
from concourse import mybir
from concourse.alu_op_type import AluOpType as ALU

FP32 = mybir.dt.float32
I32 = mybir.dt.int32
U16 = mybir.dt.uint16
BF16 = mybir.dt.bfloat16
ACT = mybir.ActivationFunctionType
AX = mybir.AxisListType
DVE_ENGINE = mybir.EngineType.DVE
PE_ENGINE = mybir.EngineType.PE
POOL_ENGINE = mybir.EngineType.Pool
ACT_ENGINE = mybir.EngineType.Activation
SP_ENGINE = mybir.EngineType.SP

P = 128
NODES, EDGES, D, HEADS = 12500, 212500, 96, 8
HD = D // HEADS
NT = -(-NODES // P)
ET = -(-EDGES // P)
G = 4
RING = 4
BODY = G * RING
TURNS = -(-(ET + NT - 1) // BODY)
SCOLS = -(-((TURNS + 1) * BODY) // P)
STEPS = SCOLS * P
W0 = 2 * D
W1 = D + HEADS
C = 7
CHUNKS = NT // C
BLOCKS = 7
BT = NT // BLOCKS
TINY = 1e-37
LIMIT = 64.0
ORDERED_TILES = ET
EPS_MSG, EPS_LN, EPS_Z, CLIP = 1e-7, 1e-5, 1e-6, 5.0


def build(nc, x, ids, dst_last, dst_line, edge_t, w0, wqkv, we, out):
    ctx = ExitStack()
    with ctx:
        def sb(name, shape, dt=FP32):
            return ctx.enter_context(nc.sbuf_tensor(name, shape, dt))

        def ps(name, shape, dt=FP32):
            return ctx.enter_context(nc.psum_tensor(name, shape, dt))

        def sem(name):
            return ctx.enter_context(nc.semaphore(name))

        table0 = nc.dram_tensor("table0", (NT * P, W0), FP32, kind="Internal").ap()
        table1 = nc.dram_tensor("table1", (NT * P, 2 * D), FP32, kind="Internal").ap()
        steps_dram = nc.dram_tensor("steps_dram", (4, STEPS), I32, kind="Internal").ap()

        state0 = nc.dram_tensor("state0", (NT * P, 3 * D), FP32, kind="Internal").ap()
        message = nc.dram_tensor("message", (NT * P, D), FP32, kind="Internal").ap()
        query = nc.dram_tensor("query", (NT * P, D), FP32, kind="Internal").ap()
        key_value = nc.dram_tensor("key_value", (NT * P, 2 * D), FP32, kind="Internal").ap()
        state1 = nc.dram_tensor("state1", (NT * P, W1), FP32, kind="Internal").ap()
        projection = nc.dram_tensor("projection", (P, D), FP32, kind="Internal").ap()

        xs = sb("xs", [P, NT, D])
        sums = sb("sums", [P, NT * W0])
        qs = sb("qs", [P, NT * D])
        rows = sb("rows", [P, RING, G, W0])
        onehot = sb("onehot", [P, RING, G, P])
        score = sb("score", [P, G, HEADS])
        idx = sb("idx", [P, RING, G], I32)
        src_t = sb("src_t", [P, STEPS], U16)
        rel_t = sb("rel_t", [P, STEPS], BF16)
        step_tab = sb("step_tab", [4, STEPS], I32)
        iota_n = sb("iota_n", [P, P])
        ident = sb("ident", [P, P])
        w0_sb = sb("w0_sb", [D + 1, D])
        wqkv_sb = sb("wqkv_sb", [D + 1, 3 * D])
        we_sb = sb("we_sb", [D + 1, D])
        xt = sb("xt", [D + 1, 2, C * P])
        ys = sb("ys", [P, 2, C, D])
        feat1 = sb("feat1", [P, C * D])
        bn = sb("bn", [P, C, 6])
        mv = sb("mv", [P, C, 2])
        std = sb("std", [P, C])
        scale = sb("scale", [P, 2, C, 2])
        zr = sb("zr", [P, 2, C, HEADS])
        xmax = sb("xmax", [P, BLOCKS])
        gmax = sb("gmax", [P, 3])
        bad = sb("bad", [P, 3])
        flag = sb("flag", [1, 1], I32)

        used = [0]

        def carve(home, shape, dt=FP32, parts=P):
            n = 1
            for c in shape:
                n *= c
            t = home[0:parts, used[0]:used[0] + n]
            used[0] += n
            if dt != FP32:
                t = t.bitcast(dt)
            if len(shape) == 2:
                t = t.rearrange("p (a b) -> p a b", b=shape[1])
            if len(shape) == 3:
                t = t.rearrange("p (a b c) -> p a b c", b=shape[1], c=shape[2])
            return t

        ids_g = carve(qs, [SCOLS, 2 * P], I32)
        rel_s = carve(qs, [SCOLS, P])
        src_s = carve(qs, [SCOLS, P])
        hit = carve(qs, [ET])
        iota_e = hit.bitcast(I32)
        dst_next = hit.bitcast(I32)
        small = carve(qs, [5, SCOLS])
        pack = carve(qs, [4, SCOLS])
        pack_i = carve(qs, [P], I32, 4 * SCOLS)
        step_i = carve(qs, [SCOLS], I32)
        iota_p = carve(qs, [P], I32)
        iota_s = carve(qs, [SCOLS], I32)
        assert used[0] <= NT * D
        last_i = rows[:, :, :, :].rearrange("p a b c -> p (a b c)")[:, 0:ET].bitcast(I32)
        end_step = onehot[:, :, :, :].rearrange("p a b c -> p (a b c)")[:, 0:ET]
        dst_here = end_step.bitcast(I32)
        node_tile = rows[:, :, :, :].rearrange("p a b c -> p (a b c)")[:, 0:STEPS].bitcast(I32).rearrange(
            "p (j c) -> p j c", c=P)
        line = ys[0:1, :, :, :].rearrange("p a b c -> p (a b c)")
        e_ids = line[:, 0:2 * P].bitcast(I32)
        e_state, e_row, e_diff, e_query, e_proj, e_prod = (
            line[:, lo * D:hi * D] for lo, hi in ((3, 6), (6, 8), (8, 10), (10, 11), (11, 12), (12, 13)))
        used[0] = NT * W1
        ea = carve(sums, [RING, G, P], parts=D + 1)
        onehot_t = carve(sums, [2, G, P])
        vals = carve(sums, [2, G, W1])
        prod = carve(sums, [G, D])
        assert used[0] <= NT * W0

        sums0 = sums[:, :].rearrange("p (k c) -> p k c", c=W0)
        sums1 = sums[:, 0:NT * W1].rearrange("p (k c) -> p k c", c=W1)
        rows_flat = rows[:, :, :, :].rearrange("p a b c -> p (a b c)")
        onehot_flat = onehot[:, :, :, :].rearrange("p a b c -> p (a b c)")
        qkv = [t[:, 0:C * 3 * D].rearrange("p (k c) -> p k c", c=3 * D) for t in (rows_flat, onehot_flat)]
        feat = [t.rearrange("p (k c) -> p k c", c=D)
                for t in (rows_flat[:, C * 3 * D:C * 4 * D], feat1[:, :])]
        quot, done = ([rows_flat[:, (2 * a + b) * C * D:(2 * a + b + 1) * C * D].rearrange("p (k c) -> p k c", c=D)
                       for b in range(2)] for a in range(2))

        banks = ps("banks", [P, 8, 512])
        flat = banks[:, :, :].rearrange("p a b -> p (a b)")
        ps_sum0 = [banks[:, 2 * b:2 * b + 2, :].rearrange("p a (c d) -> p a c d", d=256) for b in range(2)]
        ps_trf = flat[0:D, 6 * 512:6 * 512 + C * P]
        ps_try = flat[0:D, 0:C * P]
        ps_h = banks[:, 2:4, :]
        ps_qkv = [banks[:, 4 + u % 2, 0:3 * D] for u in range(C)]
        ps_e = [banks[:, b, 0:G * D] for b in range(2)]
        ps_q = [banks[:, 2 + b, 0:G * D] for b in range(2)]
        ps_t = banks[:, 4, :].rearrange("p (a b) -> p a b", b=P)
        ps_sum1 = [banks[:, 5 + b, 0:G * W1].rearrange("p (a b) -> p a b", b=W1) for b in range(2)]
        ps_misc = banks[:, 7, :]

        s_last = sem("s_last")
        s_x = [sem(f"s_xin{b}") for b in range(BLOCKS)]
        s_w = sem("s_w")
        s_iota = sem("s_iota")
        s_wq = sem("s_wq")
        s_dve = sem("s_dve")
        s_step = sem("s_step")
        s_ids = sem("s_ids")
        s_tin = sem("s_tin")
        s_tps = sem("s_tps")
        s_tcp = sem("s_tcp")
        s_pack = sem("s_pack")
        s_tab = sem("s_tab")
        s_gm = sem("s_gm")
        s_gall = sem("s_gall")
        s_gneg = sem("s_gneg")
        s_relu = sem("s_relu")
        s_exp0 = sem("s_exp0")
        s_t0 = sem("s_t0")
        s_t0w = [sem(f"s_t0w{b}") for b in range(BLOCKS)]
        s_dst = sem("s_dst")
        s_bad = sem("s_bad")
        s_ball = sem("s_ball")
        s_flag = sem("s_flag")
        s_prep = sem("s_prep")
        s_msg = sem("s_msg")
        s_eids = sem("s_eids")
        s_eids1 = sem("s_eids1")
        s_load = sem("s_load")
        s_one = sem("s_one")
        s_diff = sem("s_diff")
        s_eexp = sem("s_eexp")
        s_new = sem("s_new")
        s_store = sem("s_store")
        s_back = sem("s_back")
        s_prep1 = sem("s_prep1")
        s_tin1 = sem("s_tin1")
        s_proj = sem("s_proj")
        s_pcp = sem("s_pcp")
        s_pst = sem("s_pst")
        s_load1 = sem("s_load1")
        s_one1 = sem("s_one1")
        s_clip1 = sem("s_clip1")
        s_eexp1 = sem("s_eexp1")
        s_new1 = sem("s_new1")
        s_store1 = sem("s_store1")
        s_back1 = sem("s_back1")
        s_slot = sem("s_slot")
        s_rows = [sem(f"s_rows{r}") for r in range(RING)]
        s_hot = sem("s_hot")
        s_sum = sem("s_sum")
        s_add = sem("s_add")
        s_fch = sem("s_fch")
        s_feat = sem("s_feat")
        s_ftr = sem("s_ftr")
        s_ft = sem("s_ft")
        s_h = sem("s_h")
        s_y = sem("s_y")
        s_bn = sem("s_bn")
        s_ag = sem("s_ag")
        s_var = sem("s_var")
        s_std = sem("s_std")
        s_rec = sem("s_rec")
        s_scale = sem("s_scale")
        s_x1 = sem("s_x1")
        s_xcp = sem("s_xcp")
        s_ytr = sem("s_ytr")
        s_yt = sem("s_yt")
        s_qkv = sem("s_qkv")
        s_qcp = sem("s_qcp")
        s_ev = sem("s_ev")
        s_kvw = [sem(f"s_kvw{r}") for r in range(2)]
        s_zero = sem("s_zero")
        s_ones = sem("s_ones")
        s_slot1 = sem("s_slot1")
        s_rows1 = [sem(f"s_rows1_{r}") for r in range(RING)]
        s_ea = [sem(f"s_ea{r}") for r in range(RING)]
        s_hot1 = sem("s_hot1")
        s_tr = sem("s_tr")
        s_trc = sem("s_trc")
        s_eu = sem("s_eu")
        s_qe = sem("s_qe")
        s_mid = sem("s_mid")
        s_clip = sem("s_clip")
        s_exp1 = sem("s_exp1")
        s_vals = sem("s_vals")
        s_sum1 = sem("s_sum1")
        s_add1 = sem("s_add1")
        s_zch = sem("s_zch")
        s_out1 = sem("s_out1")
        s_y1 = sem("s_y1")
        s_bn1 = sem("s_bn1")
        s_ag1 = sem("s_ag1")
        s_var1 = sem("s_var1")
        s_std1 = sem("s_std1")
        s_rec1 = sem("s_rec1")
        s_scale1 = sem("s_scale1")
        s_y2 = sem("s_y2")
        s_out = [sem(f"s_stored{b}") for b in range(2)]

        nodes = "(k p) c -> p k c"
        parts = "(p k) c -> p k c"
        why = "the step table is clamped to the tiles when it is made"

        def step_values(engine, row, at, top):
            return nc.values_load_multi_w_load_instructions(
                step_tab[row:row + 1, bass.ds(at, G)], engines=[engine], min_val=0, max_val=top,
                skip_runtime_bounds_check_because=why)[1]

        qs_tiles = qs[:, :].rearrange("p (k c) -> p k c", c=D)

        def tiles(t, k, n):
            return t[:, k:k + n, :] if isinstance(k, int) else t[:, bass.ds(k, n), :]

        def chunk_loop(engine, part):
            for c in range(4):
                part(c, c % 2, c // 2, True, c >= 1, c >= 2)
            with engine.Fori(0, (CHUNKS - 4) // 2) as i:
                for b in range(2):
                    part(i * 2 + (4 + b), b, i + 2, True, True, True)
            part(CHUNKS, 0, CHUNKS // 2, False, True, True)
            part(CHUNKS + 1, 1, CHUNKS // 2, False, False, True)

        def irregular(engine, kind):
            engine.wait_ge(s_flag, 1)
            return nc.values_load_multi_w_load_instructions(
                flag[0:1, 0:1], engines=[kind], min_val=0, max_val=1,
                skip_runtime_bounds_check_because="it is 0 or 1")[1][0]

        block = ctx.enter_context(nc.Block())

        @block.sync
        def _(sp):
            sp.dma_start(last_i, dst_last.to_broadcast([P, ET])).then_inc(s_last, 16)
            for b in range(BLOCKS):
                sp.dma_start(xs[:, b * BT:(b + 1) * BT, :], x[:, b * BT:(b + 1) * BT, :]).then_inc(s_x[b], 16)
            sp.dma_start(w0_sb[:, :], w0).then_inc(s_w, 16)
            sp.dma_start(wqkv_sb[:, :], wqkv).then_inc(s_w, 16)
            sp.dma_start(we_sb[:, :], we).then_inc(s_w, 16)
            sp.wait_ge(s_step, 1)
            sp.dma_start(dst_here, dst_line[0:ET * P].rearrange("(p j) -> p j", p=P)).then_inc(s_dst, 16)
            sp.dma_start(dst_next, dst_line[1:ET * P + 1].rearrange("(p j) -> p j", p=P)).then_inc(s_dst, 16)
            for b in range(BLOCKS):
                sp.wait_ge(s_t0, b + 1)
                sp.dma_start(table0.rearrange(parts, p=P)[:, b * BT:(b + 1) * BT],
                             sums0[:, b * BT:(b + 1) * BT]).then_inc(s_t0w[b], 16)
            sp.wait_ge(s_pack, 1)
            sp.dma_start(steps_dram.rearrange("q (j s) -> (q j) s", s=P), pack_i).then_inc(s_tab, 16)
            sp.wait_ge(s_tab, 16)
            sp.dma_start(step_tab[:, :], steps_dram).then_inc(s_tab, 16)
            def edge_by_edge(tables, s_edge, s_loaded, s_done, s_stored, state, new_state, before_tile=None):
                with sp.Fori(0, ORDERED_TILES) as t:
                    sp.dma_start(e_ids, ids[bass.ds(t, 1), :]).then_inc(s_edge, 16)
                    sp.wait_ge(s_edge, t * 16 + 16)
                    sp.nop(nofuse=True)
                    if before_tile:
                        before_tile(t)
                    with sp.Fori(0, P) as u:
                        src, dst = (nc.values_load_multi_w_load_instructions(
                            e_ids[0:1, bass.ds(u + lo, 1)], engines=[SP_ENGINE], min_val=0, max_val=NT * P - 1,
                            skip_runtime_bounds_check_because="ids are node numbers")[1][0] for lo in (0, P))
                        rows_of = {"src": src, "dst": dst, "edge": u}
                        for to, table, which in tables:
                            sp.dma_start(to, table[bass.ds(rows_of[which], 1), :]).then_inc(s_loaded, 16)
                        sp.wait_ge(s_done, t * P + u + 1)
                        sp.nop(nofuse=True)
                        sp.dma_start(state[bass.ds(dst, 1), :], new_state).then_inc(s_stored, 16)
                        sp.wait_ge(s_stored, t * (16 * P) + u * 16 + 16)
                        sp.nop(nofuse=True)

            with sp.If(irregular(sp, SP_ENGINE)):
                sp.wait_ge(s_add, 1)
                sp.dma_start(state0[:, 0:2 * D].rearrange(nodes, p=P), sums0).then_inc(s_prep, 16)
                sp.dma_start(state0[:, 2 * D:3 * D].rearrange(nodes, p=P), sums0[:, :, 0:D]).then_inc(s_prep, 16)
                sp.wait_ge(s_prep, 32)
                sp.wait_ge(s_msg, 1)
                sp.dma_start(message.rearrange(nodes, p=P), qs_tiles).then_inc(s_prep, 16)
                sp.wait_ge(s_prep, 48)
                edge_by_edge([(e_row[:, 0:D], message, "src"), (e_state, state0, "dst")], s_eids, s_load, s_new,
                             s_store, state0, e_state)
                sp.dma_start(sums0, state0[:, D:3 * D].rearrange(nodes, p=P)).then_inc(s_back, 16)
            with sp.Fori(0, CHUNKS // 2) as i:
                for b in range(2):
                    sp.wait_ge(s_ev, i * (2 * C) + (b + 1) * C)
                    sp.dma_start(table1.rearrange(parts, p=P)[:, bass.ds(i * (2 * C) + b * C, C)],
                                 qkv[b][:, :, D:3 * D]).then_inc(s_kvw[b], 16)
            def load_edges(at, r):
                for u, tile in enumerate(step_values(SP_ENGINE, 3, at, ET - 1)):
                    sp.dma_start(ea[0:D, r, u, :],
                                 edge_t[bass.ds(tile, 1)].rearrange("a c e -> (a c) e")).then_inc(s_ea[r], 16)
            with sp.If(1 - irregular(sp, SP_ENGINE)):
                sp.wait_ge(s_ones, 1)
                for r in range(RING):
                    load_edges(r * G, r)
                with sp.Fori(0, TURNS) as i:
                    for r in range(RING):
                        sp.wait_ge(s_eu, i * RING + (r + 1))
                        load_edges(i * BODY + (BODY + r * G), r)
                for r in range(RING):
                    sp.wait_ge(s_ea[r], 16 * G * (TURNS + 1))
            with sp.If(irregular(sp, SP_ENGINE)):
                sp.wait_ge(s_zero, 1)
                sp.wait_ge(s_ones, 1)
                sp.wait_ge(s_qcp, CHUNKS)
                for b in range(2):
                    sp.wait_ge(s_kvw[b], 16 * (CHUNKS // 2))
                sp.dma_start(state1.rearrange(nodes, p=P), sums1).then_inc(s_prep1, 16)
                sp.dma_start(query.rearrange(nodes, p=P), qs_tiles).then_inc(s_prep1, 16)
                sp.dma_start(key_value.rearrange(nodes, p=P), table1.rearrange(parts, p=P)).then_inc(s_prep1, 16)
                sp.wait_ge(s_prep1, 48)

                def project(t):
                    sp.dma_start(ea[0:D, 0, 0, :], edge_t[bass.ds(t, 1)].rearrange("a c e -> (a c) e")).then_inc(s_tin1, 16)
                    sp.wait_ge(s_pcp, t + 1)
                    sp.nop(nofuse=True)
                    sp.dma_start(projection, rows[:, 0, 0, 0:D]).then_inc(s_pst, 16)
                    sp.wait_ge(s_pst, t * 16 + 16)
                    sp.nop(nofuse=True)

                edge_by_edge([(e_row, key_value, "src"), (e_query, query, "dst"), (e_state[:, 0:W1], state1, "dst"),
                              (e_proj, projection, "edge")], s_eids1, s_load1, s_new1, s_store1, state1,
                             e_state[:, 0:W1], project)
                sp.dma_start(sums1, state1.rearrange(nodes, p=P)).then_inc(s_back1, 16)
            with sp.Fori(0, CHUNKS // 2) as i:
                for b in range(2):
                    sp.wait_ge(s_y2, i * 2 + (b + 1))
                    sp.dma_start(out[:, bass.ds(i * (2 * C) + b * C, C)], done[b]).then_inc(s_out[b], 16)
            for b in range(2):
                sp.wait_ge(s_out[b], 16 * (CHUNKS // 2))

        @block.gpsimd
        def _(pool):
            pool.iota(iota_e, pattern=[[1, ET]], base=0, channel_multiplier=0).then_inc(s_iota, 1)
            pool.iota(iota_p, pattern=[[1, P]], base=0, channel_multiplier=0).then_inc(s_iota, 1)
            pool.iota(iota_s, pattern=[[P, SCOLS]], base=0, channel_multiplier=1).then_inc(s_iota, 1)
            pool.wait_ge(s_iota, 3)
            pool.memset(xt[D:D + 1, :, :], 1.0).then_inc(s_iota, 1)
            pool.wait_ge(s_iota, 4)
            pool.memset(ident[:, :], 1.0).then_inc(s_iota, 1)
            pool.wait_ge(s_iota, 5)
            pool.affine_select(out=ident[:, :], in_=ident[:, :], compare_op=ALU.is_equal, fill=0.0,
                               base=0, pattern=[[-1, P]], channel_multiplier=1).then_inc(s_iota, 1)
            pool.wait_ge(s_step, 1)
            for j in range(SCOLS):
                pool.indirect_dma_start(out=ids_g[:, j, :], out_offset=None, in_=ids,
                                        in_offset=bass.IndirectOffsetOnAxis(ap=step_i[:, j:j + 1], axis=0)
                                        ).then_inc(s_ids, 16)
            pool.wait_ge(s_gm, 1)
            pool.partition_all_reduce(gmax[:, 1:2], gmax[:, 0:1], P, bass.bass_isa.ReduceOp.max).then_inc(s_gall, 1)
            pool.wait_ge(s_bad, 1)
            pool.partition_all_reduce(bad[:, 2:3], bad[:, 1:2], P, bass.bass_isa.ReduceOp.max).then_inc(s_ball, 1)
            for b in range(BLOCKS):
                pool.wait_ge(s_t0w[b], 16)
            with pool.If(1 - irregular(pool, POOL_ENGINE)):
                with pool.Fori(0, TURNS) as i:
                    for r in range(RING):
                        pool.wait_ge(s_slot, i * RING + (r + 1))
                        pool.nop(nofuse=True)
                        for u in range(G):
                            pool.indirect_dma_start(out=rows[:, r, u, :], out_offset=None, in_=table0,
                                                    in_offset=bass.IndirectOffsetOnAxis(ap=idx[:, r, u:u + 1], axis=0)
                                                    ).then_inc(s_rows[r], 16)
            def keep(c, b, half, enters, norms, leaves):
                if leaves:
                    pool.wait_ge(s_ev, (c - 1) * C)
                    pool.nop(nofuse=True)
                    pool.tensor_copy(tiles(qs_tiles, (c - 2) * C, C), qkv[b][:, :, 0:D]).then_inc(s_qcp, 1)
                if norms:
                    pool.wait_ge(s_x1, c)
                    pool.nop(nofuse=True)
                    pool.tensor_copy(tiles(xs, (c - 1) * C, C), ys[:, 1 - b]).then_inc(s_xcp, 1)
                if not enters and norms:
                    pool.memset(sums[:, 0:NT * W1], 0.0).then_inc(s_zero, 1)
                    pool.wait_ge(s_zero, 1)
                    pool.memset(ea[D:D + 1, :, :, :], 1.0).then_inc(s_ones, 1)
                    pool.wait_ge(s_ones, 1)
            chunk_loop(pool, keep)
            for b in range(2):
                pool.wait_ge(s_kvw[b], 16 * (CHUNKS // 2))
            with pool.If(1 - irregular(pool, POOL_ENGINE)):
                with pool.Fori(0, TURNS) as i:
                    for r in range(RING):
                        pool.wait_ge(s_slot1, i * RING + (r + 1))
                        pool.nop(nofuse=True)
                        for u in range(G):
                            pool.indirect_dma_start(out=rows[:, r, u, :], out_offset=None, in_=table1,
                                                    in_offset=bass.IndirectOffsetOnAxis(ap=idx[:, r, u:u + 1], axis=0)
                                                    ).then_inc(s_rows1[r], 16)

            def residual(c, b):
                pool.wait_ge(s_out1, c + 1)
                pool.nop(nofuse=True)
                if not isinstance(c, int):
                    pool.wait_ge(s_y2, c - 1)
                    pool.nop(nofuse=True)
                pool.tensor_tensor(ys[:, b], quot[b], tiles(xs, c * C, C), ALU.add).then_inc(s_y1, 1)
            for b in range(2):
                residual(b, b)
            with pool.Fori(1, CHUNKS // 2) as i:
                for b in range(2):
                    residual(i * 2 + b, b)

        @block.tensor
        def _(pe):
            pe.wait_ge(s_iota, 6)
            for c in range(2 * SCOLS // 4 + 1):
                if c < 2 * SCOLS // 4:
                    pe.wait_ge(s_tin, 1 + (4 * c >= SCOLS))
                    if c:
                        pe.wait_ge(s_tcp, c)
                    for u in range(4):
                        n = 4 * c + u
                        m = rel_s[:, n, :] if n < SCOLS else src_s[:, n - SCOLS, :]
                        last = nc.tensor.transpose(ps_misc[:, u * P:(u + 1) * P], m, ident[:, :])
                    last.then_inc(s_tps, 1)
                else:
                    pe.wait_ge(s_tcp, c)
                    nc.tensor.transpose(ps_misc[0:4 * SCOLS, 0:P], pack[:, :, :].rearrange("p q j -> p (q j)"),
                                        ident[:, :]).then_inc(s_tps, 1)

            with pe.If(1 - irregular(pe, PE_ENGINE)):
                with pe.Fori(0, TURNS) as i:
                    for r in range(RING):
                        pe.wait_ge(s_hot, i * RING + (r + 1))
                        pe.wait_ge(s_rows[r], i * (16 * G) + 16 * G)
                        for u in range(G):
                            last = nc.tensor.matmul(ps_sum0[r % 2][:, u // 2, u % 2, 0:W0], onehot[:, r, u, :],
                                                    rows[:, r, u, :], start=True, stop=True)
                        last.then_inc(s_sum, 1)

            def products(c, b, half, enters, norms, leaves):
                if leaves:
                    pe.wait_ge(s_x1, c - 1)
                    for u in range(C):
                        last = nc.tensor.transpose(ps_try[:, u * P:(u + 1) * P], ys[:, b, u, :], ident[:, :])
                    last.then_inc(s_ytr, 1)
                if enters:
                    pe.wait_ge(s_feat, c + 1)
                    for u in range(C):
                        last = nc.tensor.transpose(ps_trf[:, u * P:(u + 1) * P], feat[b][:, u, :], ident[:, :])
                    last.then_inc(s_ftr, 1)
                if leaves:
                    pe.wait_ge(s_yt, c - 1)
                    for u in range(C):
                        if u >= 2:
                            pe.wait_ge(s_ev, (c - 2) * C + (u - 1))
                        nc.tensor.matmul(ps_qkv[u], xt[:, 1, u * P:(u + 1) * P], wqkv_sb[:, :],
                                         start=True, stop=True).then_inc(s_qkv, 1)
                if enters:
                    pe.wait_ge(s_ft, c + 1)
                    if norms:
                        pe.wait_ge(s_y, c)
                    for u in range(C):
                        last = nc.tensor.matmul(ps_h[:, u // 4, (u % 4) * D:(u % 4 + 1) * D],
                                                xt[:, 0, u * P:(u + 1) * P], w0_sb[:, :], start=True, stop=True)
                    last.then_inc(s_h, 1)

            pe.wait_ge(s_wq, 1)
            chunk_loop(pe, products)

            def scores_ahead(at, r, n, turn):
                pe.wait_ge(s_hot1, n)
                for u in range(G):
                    last = nc.tensor.transpose(ps_t[:, u, :], onehot[:, r, u, :], ident[:, :])
                last.then_inc(s_tr, 1)
                pe.wait_ge(s_ea[r], turn)
                for u in range(G):
                    last = nc.tensor.matmul(ps_e[r % 2][:, u * D:(u + 1) * D], ea[:, r, u, :], we_sb[:, :],
                                            start=True, stop=True)
                last.then_inc(s_eu, 1)
                offs = step_values(PE_ENGINE, 2, at, (NT - 1) * D)
                pe.wait_ge(s_trc, n)
                for u in range(G):
                    last = nc.tensor.matmul(ps_q[r % 2][:, u * D:(u + 1) * D], onehot_t[:, r % 2, u, :],
                                            qs[:, bass.ds(offs[u], D)], start=True, stop=True)
                last.then_inc(s_qe, 1)

            def sum_values(r, n):
                pe.wait_ge(s_vals, n)
                for u in range(G):
                    last = nc.tensor.matmul(ps_sum1[r % 2][:, u, :], onehot[:, r, u, :], vals[:, r % 2, u, :],
                                            start=True, stop=True)
                last.then_inc(s_sum1, 1)

            pe.wait_ge(s_tab, 32)
            pe.wait_ge(s_ones, 1)
            pe.wait_ge(s_ev, NT)
            pe.wait_ge(s_qcp, CHUNKS)
            with pe.If(1 - irregular(pe, PE_ENGINE)):
                scores_ahead(0, 0, 1, 16 * G)
                for r in range(RING):
                    if r:
                        sum_values(r - 1, r)
                    scores_ahead((r + 1) * G, (r + 1) % RING, r + 2, 16 * G * (1 + (r == RING - 1)))
                with pe.Fori(1, TURNS) as i:
                    for r in range(RING):
                        sum_values((r - 1) % RING, i * RING + r)
                        scores_ahead(i * BODY + (r + 1) * G, (r + 1) % RING, i * RING + (r + 2),
                                     i * (16 * G) + 16 * G * (1 + (r == RING - 1)))
                sum_values(RING - 1, TURNS * RING)
            with pe.If(irregular(pe, PE_ENGINE)):
                with pe.Fori(0, ORDERED_TILES) as t:
                    pe.wait_ge(s_tin1, t * 16 + 16)
                    nc.tensor.matmul(ps_e[0][:, 0:D], ea[:, 0, 0, :], we_sb[:, :], start=True,
                                     stop=True).then_inc(s_proj, 1)

        @block.scalar
        def _(act):
            for b in range(BLOCKS):
                act.wait_ge(s_x[b], 16)
                nc.scalar.activation(sums0[:, b * BT:(b + 1) * BT, D:W0], xs[:, b * BT:(b + 1) * BT],
                                     ACT.Relu).then_inc(s_relu, 1)
            act.wait_ge(s_gneg, 1)
            for b in range(BLOCKS):
                act.wait_ge(s_relu, b + 1)
                nc.scalar.activation(sums0[:, b * BT:(b + 1) * BT, 0:D], sums0[:, b * BT:(b + 1) * BT, D:W0],
                                     ACT.Exp, bias=gmax[:, 2:3]).then_inc(s_exp0, 1)

            def chunk(c, b, half, enters, norms, leaves):
                if leaves:
                    act.wait_ge(s_ytr, c - 1)
                    nc.scalar.copy(xt[0:D, 1, :], ps_try).then_inc(s_yt, 1)
                if enters:
                    act.wait_ge(s_ftr, c + 1)
                    nc.scalar.copy(xt[0:D, 0, :], ps_trf).then_inc(s_ft, 1)
                if leaves and (not isinstance(c, int) or c >= 4):
                    act.wait_ge(s_kvw[b], (half - 1) * 16)
                    act.wait_ge(s_qcp, c - 3)
                for u in range(C):
                    if leaves:
                        act.wait_ge(s_qkv, (c - 2) * C + (u + 1))
                        nc.scalar.copy(qkv[b][:, u, :], ps_qkv[u]).then_inc(s_ev, 1)
                    if norms and u == 3:
                        act.wait_ge(s_var, c)
                        nc.scalar.activation(std[:, :], mv[:, :, 1], ACT.Sqrt).then_inc(s_std, 1)
                if norms:
                    act.wait_ge(s_scale, c)
                    for u in range(C):
                        y = ys[:, 1 - b, u, :]
                        last = nc.scalar.activation(y, y, ACT.Identity, bias=scale[:, 1 - b, u, 1:2],
                                                    scale=scale[:, 1 - b, u, 0:1])
                    last.then_inc(s_x1, 1)

            with act.If(irregular(act, ACT_ENGINE)):
                with act.Fori(0, ORDERED_TILES * P) as n:
                    act.wait_ge(s_diff, n + 1)
                    nc.scalar.activation(e_diff, e_diff, ACT.Exp).then_inc(s_eexp, 1)

            chunk_loop(act, chunk)

            def copy_onehot(b, n):
                act.wait_ge(s_tr, n)
                nc.scalar.copy(onehot_t[:, b, :, :], ps_t[:, :, :]).then_inc(s_trc, 1)

            with act.If(1 - irregular(act, ACT_ENGINE)):
                copy_onehot(0, 1)
                with act.Fori(0, TURNS) as i:
                    for r in range(RING):
                        copy_onehot((r + 1) % 2, i * RING + (r + 2))
                        act.wait_ge(s_clip, i * RING + (r + 1))
                        nc.scalar.activation(vals[:, r % 2, :, D:W1], score[:, :, :], ACT.Exp).then_inc(s_exp1, 1)
            with act.If(irregular(act, ACT_ENGINE)):
                with act.Fori(0, ORDERED_TILES) as t:
                    act.wait_ge(s_proj, t + 1)
                    nc.scalar.copy(rows[:, 0, 0, 0:D], ps_e[0][:, 0:D]).then_inc(s_pcp, 1)
                    with act.Fori(0, P) as u:
                        act.wait_ge(s_clip1, t * P + u + 1)
                        nc.scalar.activation(e_prod[:, 0:HEADS], e_prod[:, 0:HEADS], ACT.Exp).then_inc(s_eexp1, 1)
            def norm(c, b, half):
                act.wait_ge(s_var1, c + 1)
                nc.scalar.activation(std[:, :], mv[:, :, 1], ACT.Sqrt).then_inc(s_std1, 1)
                if half is not None:
                    act.wait_ge(s_out[b], half * 16)
                act.wait_ge(s_scale1, c + 1)
                for u in range(C):
                    last = nc.scalar.activation(done[b][:, u, :], ys[:, b, u, :], ACT.Identity,
                                                bias=scale[:, b, u, 1:2], scale=scale[:, b, u, 0:1])
                last.then_inc(s_y2, 1)
            for b in range(2):
                norm(b, b, None)
            with act.Fori(1, CHUNKS // 2) as i:
                for b in range(2):
                    norm(i * 2 + b, b, i)

        @block.vector
        def _(dve):
            chain = [0]

            def link(ins):
                chain[0] += 1
                ins.then_inc(s_dve, 1)
                dve.wait_ge(s_dve, chain[0])

            V = nc.vector
            cnt, kf, pen, kc = small[:, 0, :], small[:, 1, :], small[:, 2, :], small[:, 3, :]
            stepf = small[:, 4, :]
            dve.wait_ge(s_last, 16)
            dve.wait_ge(s_iota, 6)
            link(V.tensor_scalar(last_i, last_i, 7, None, ALU.logical_shift_right))
            link(V.tensor_copy(end_step, iota_e))
            link(V.tensor_tensor(end_step, end_step, last_i, ALU.add))
            V.tensor_copy(iota_n[:, :], iota_p)
            link(V.tensor_copy(stepf, iota_s))

            def count_ended(j):
                link(V.tensor_scalar(hit, end_step, stepf[:, j:j + 1], None, ALU.is_lt, ALU.add,
                                     accum_out=cnt[:, j:j + 1]))

            for j in range(SCOLS):
                count_ended(j)
            link(V.tensor_scalar(pack[:, 3, :], cnt, float(ET - 1), None, ALU.min))
            V.tensor_copy(step_i, pack[:, 3, :]).then_inc(s_step, 1)
            for b in range(BLOCKS):
                dve.wait_ge(s_x[b], 16)
                last = V.tensor_reduce(xmax[:, b:b + 1], xs[:, b * BT:(b + 1) * BT, :], AX.XY, ALU.max)
            link(last)
            V.tensor_reduce(gmax[:, 0:1], xmax[:, :], AX.X, ALU.max).then_inc(s_gm, 1)
            link(V.tensor_tensor(kf, stepf, cnt, ALU.subtract))
            link(V.tensor_scalar(pen, cnt, float(ET), 1.0e6, ALU.is_ge, ALU.mult))
            link(V.tensor_scalar(kc, kf, float(NT - 1), None, ALU.min))
            V.tensor_scalar(pack[:, 0, :], kc, float(W0), None, ALU.mult)
            V.tensor_scalar(pack[:, 1, :], kc, float(W1), None, ALU.mult)
            V.tensor_scalar(pack[:, 2, :], kc, float(D), None, ALU.mult)
            link(V.tensor_scalar(kf, kf, float(P), None, ALU.mult))
            link(V.tensor_tensor(kf, kf, pen, ALU.add))
            dve.wait_ge(s_gall, 1)
            V.tensor_scalar(gmax[:, 2:3], gmax[:, 1:2], 0.0, -1.0, ALU.max, ALU.mult).then_inc(s_gneg, 1)
            for b in range(BLOCKS):
                dve.wait_ge(s_exp0, b + 1)
                t = sums0[:, b * BT:(b + 1) * BT]
                V.scalar_tensor_tensor(out=t[:, :, D:W0], in0=t[:, :, D:W0], scalar=EPS_MSG, in1=t[:, :, 0:D],
                                       op0=ALU.add, op1=ALU.mult).then_inc(s_t0, 1)
            dve.wait_ge(s_ids, 16 * SCOLS)
            for j in range(SCOLS):
                last = V.tensor_scalar(rel_s[:, j, :], ids_g[:, j, P:2 * P], kf[:, j:j + 1], None, ALU.subtract)
            last.then_inc(s_tin, 1)
            node = ids_g[:, :, 0:P]
            link(V.tensor_scalar(node_tile, node, 7, None, ALU.logical_shift_right))
            link(V.scalar_tensor_tensor(out=src_s, in0=node_tile, scalar=-float(P), in1=node, op0=ALU.mult, op1=ALU.add))
            V.scalar_tensor_tensor(out=src_s, in0=src_s, scalar=float(NT), in1=node_tile, op0=ALU.mult,
                                   op1=ALU.add).then_inc(s_tin, 1)
            for c in range(2 * SCOLS // 4):
                dve.wait_ge(s_tps, c + 1)
                for half in range(2):
                    n = 4 * c + 2 * half
                    t = rel_t if n < SCOLS else src_t
                    at = (n if n < SCOLS else n - SCOLS) * P
                    last = V.tensor_copy(t[:, at:at + 2 * P], ps_misc[:, half * 2 * P:(half + 1) * 2 * P])
                last.then_inc(s_tcp, 1)
            dve.wait_ge(s_dst, 32)
            link(V.tensor_tensor(hit, dst_next, dst_here, ALU.is_lt))
            link(V.tensor_reduce(bad[:, 0:1], hit, AX.X, ALU.max))
            link(V.tensor_scalar(bad[:, 1:2], gmax[:, 1:2], LIMIT, None, ALU.is_gt))
            V.tensor_tensor(bad[:, 1:2], bad[:, 1:2], bad[:, 0:1], ALU.max).then_inc(s_bad, 1)
            dve.wait_ge(s_tps, 2 * SCOLS // 4 + 1)
            V.tensor_copy(pack_i, ps_misc[0:4 * SCOLS, 0:P]).then_inc(s_pack, 1)

            dve.wait_ge(s_w, 48)
            V.tensor_scalar(wqkv_sb[:, 0:D], wqkv_sb[:, 0:D], float(HD) ** -0.5, None, ALU.mult).then_inc(s_wq, 1)

            def fill_slot(at, r, s):
                V.tensor_copy(idx[:, r, :], src_t[:, bass.ds(at, G)] if not isinstance(at, int) else src_t[:, at:at + G]
                              ).then_inc(s, 1)

            def make_onehot(at, r, u, n, s):
                rel = rel_t[:, bass.ds(at, n)] if not isinstance(at, int) else rel_t[:, at:at + n]
                ins = V.tensor_tensor(onehot[:, r, u:u + n, :], iota_n[:, :].unsqueeze(1).to_broadcast([P, n, P]),
                                      rel.unsqueeze(2).to_broadcast([P, n, P]), ALU.is_equal)
                if s is not None:
                    ins.then_inc(s, 1)

            dve.wait_ge(s_ball, 1)
            V.tensor_copy(flag[:, :], bad[0:1, 2:3]).then_inc(s_flag, 1)
            for r in range(RING):
                fill_slot(r * G, r, s_slot)
            for r in range(2):
                make_onehot(r * G, r, 0, G, s_hot)
            for b in range(BLOCKS):
                dve.wait_ge(s_t0w[b], 16)
                last = V.memset(sums0[:, b * BT:(b + 1) * BT], 0.0)
            last.then_inc(s_add, 1)
            dve.wait_ge(s_tab, 32)
            with dve.If(1 - irregular(dve, DVE_ENGINE)):
                with dve.Fori(0, TURNS) as i:
                    for r in range(RING):
                        offs = step_values(DVE_ENGINE, 0, i * BODY + r * G, (NT - 1) * W0)
                        dve.wait_ge(s_sum, i * RING + (r + 1))
                        fill_slot(i * BODY + (BODY + r * G), r, s_slot)
                        for u in range(G):
                            dve.wait_ge(s_add, i * BODY + (r * G + u + 1))
                            acc = sums[:, bass.ds(offs[u], W0)]
                            V.tensor_tensor(acc, acc, ps_sum0[r % 2][:, u // 2, u % 2, 0:W0], ALU.add).then_inc(s_add, 1)
                            make_onehot(i * BODY + ((r + 2) * G + u), (r + 2) % RING, u, 1, s_hot if u == G - 1 else None)
                dve.wait_ge(s_add, TURNS * BODY + 1)
            with dve.If(irregular(dve, DVE_ENGINE)):
                V.tensor_scalar(qs_tiles, xs[:, :, :], 0.0, EPS_MSG, ALU.max, ALU.add).then_inc(s_msg, 1)
                top, weight, weighted = (e_state[:, k * D:(k + 1) * D] for k in range(3))
                m = e_row[:, 0:D]
                with dve.Fori(0, ORDERED_TILES * P) as n:
                    dve.wait_ge(s_load, n * 32 + 32)
                    V.tensor_tensor(e_prod, top, m, ALU.max).then_inc(s_one, 1)
                    dve.wait_ge(s_one, n * 4 + 1)
                    V.tensor_tensor(e_diff[:, 0:D], top, e_prod, ALU.subtract).then_inc(s_one, 1)
                    V.tensor_tensor(e_diff[:, D:2 * D], m, e_prod, ALU.subtract).then_inc(s_diff, 1)
                    dve.wait_ge(s_one, n * 4 + 2)
                    V.tensor_copy(top, e_prod)
                    dve.wait_ge(s_eexp, n + 1)
                    V.tensor_tensor(weight, weight, e_diff[:, 0:D], ALU.mult)
                    V.tensor_tensor(weighted, weighted, e_diff[:, 0:D], ALU.mult)
                    V.tensor_tensor(m, m, e_diff[:, D:2 * D], ALU.mult).then_inc(s_one, 1)
                    dve.wait_ge(s_one, n * 4 + 3)
                    V.tensor_tensor(weight, weight, e_diff[:, D:2 * D], ALU.add).then_inc(s_one, 1)
                    V.tensor_tensor(weighted, weighted, m, ALU.add).then_inc(s_new, 1)
                    dve.wait_ge(s_one, n * 4 + 4)
                dve.wait_ge(s_back, 16)

            def statistics(b, c, s_in, s_bn, s_ag, s_var):
                def stats():
                    dve.wait_ge(s_in, c)
                    for u in range(C):
                        last = V.bn_stats(bn[:, u, :], ys[:, b, u, :])
                    last.then_inc(s_bn, 1)

                def aggregate():
                    dve.wait_ge(s_bn, c)
                    dve.nop(nofuse=True)
                    for u in range(C):
                        last = V.bn_aggr(mv[:, u, :], bn[:, u, :])
                    last.then_inc(s_ag, 1)

                def variance():
                    dve.wait_ge(s_ag, c)
                    V.tensor_scalar(mv[:, :, 1], mv[:, :, 1], EPS_LN, None, ALU.add).then_inc(s_var, 1)
                return stats, aggregate, variance

            def scales(b, c, s_std, s_rec, s_scale):
                dve.wait_ge(s_std, c)
                V.reciprocal(scale[:, b, :, 0], std[:, :]).then_inc(s_rec, 1)
                dve.wait_ge(s_rec, c)
                V.scalar_tensor_tensor(out=scale[:, b, :, 1], in0=mv[:, :, 0], scalar=-1.0, in1=scale[:, b, :, 0],
                                       op0=ALU.mult, op1=ALU.mult).then_inc(s_scale, 1)

            def nothing():
                pass

            def chunk(c, b, half, enters, norms, leaves):
                if enters:
                    f = feat[b]
                    n = c * 3
                    t = tiles(sums0, c * C, C)
                    V.tensor_scalar(f, t[:, :, 0:D], TINY, None, ALU.max).then_inc(s_fch, 1)
                    dve.wait_ge(s_fch, n + 1)
                    V.reciprocal(f, f).then_inc(s_fch, 1)
                    dve.wait_ge(s_fch, n + 2)
                    V.tensor_tensor(f, f, t[:, :, D:W0], ALU.mult).then_inc(s_fch, 1)
                    dve.wait_ge(s_fch, n + 3)
                    V.tensor_tensor(f, f, tiles(xs, c * C, C), ALU.add).then_inc(s_feat, 1)
                if norms:
                    dve.wait_ge(s_h, c)
                    if not isinstance(c, int) or c > 2:
                        dve.wait_ge(s_xcp, c - 2)
                        dve.wait_ge(s_ytr, c - 2)
                    for lo, hi in ((0, 4), (4, C)):
                        last = V.tensor_tensor(ys[:, 1 - b, lo:hi, :], tiles(xs, (c - 1) * C + lo, hi - lo),
                                               ps_h[:, lo // 4, 0:(hi - lo) * D].rearrange("p (a b) -> p a b", b=D),
                                               ALU.add)
                    last.then_inc(s_y, 1)
                    for step in statistics(1 - b, c, s_y, s_bn, s_ag, s_var):
                        step()
                    scales(1 - b, c, s_std, s_rec, s_scale)

            chunk_loop(dve, chunk)
            V.memset(zr[:, :, :, :], 0.0).then_inc(s_add1, 1)
            dve.wait_ge(s_zero, 1)

            def add_sums(at, r, n, done):
                offs = step_values(DVE_ENGINE, 1, at, (NT - 1) * W1)

                def add(u):
                    if u == 0:
                        dve.wait_ge(s_sum1, n)
                    dve.wait_ge(s_add1, done + (u + 1))
                    acc = sums[:, bass.ds(offs[u], W1)]
                    V.tensor_tensor(acc, acc, ps_sum1[r % 2][:, u, :], ALU.add).then_inc(s_add1, 1)
                return add

            def group(at, r, n, turn, before, mid):
                add = before or (lambda u: None)
                dve.wait_ge(s_rows1[r], turn)
                dve.wait_ge(s_qe, n)
                V.tensor_tensor(prod[:, :, :], rows[:, r, :, 0:D], ps_q[r % 2].rearrange("p (a b) -> p a b", b=D),
                                ALU.mult).then_inc(s_mid, 1)
                add(0)
                dve.wait_ge(s_mid, mid + 1)
                V.tensor_tensor(prod[:, :, :], prod[:, :, :], ps_e[r % 2].rearrange("p (a b) -> p a b", b=D),
                                ALU.mult).then_inc(s_mid, 1)
                add(1)
                dve.wait_ge(s_mid, mid + 2)
                V.tensor_reduce(score[:, :, :], prod[:, :, :].rearrange("p a (h d) -> p (a h) d", d=HD), AX.X,
                                ALU.add).then_inc(s_mid, 1)
                add(2)
                dve.wait_ge(s_mid, mid + 3)
                V.tensor_scalar(score[:, :, :], score[:, :, :], -CLIP, CLIP, ALU.max, ALU.min).then_inc(s_clip, 1)
                add(3)
                make_onehot(at + 2 * G, (r + 2) % RING, 0, G, s_hot1)
                dve.wait_ge(s_exp1, n)
                V.tensor_tensor(vals[:, r % 2, :, 0:D].rearrange("p a (h d) -> p a h d", d=HD),
                                rows[:, r, :, D:2 * D].rearrange("p a (h d) -> p a h d", d=HD),
                                vals[:, r % 2, :, D:W1].unsqueeze(3).to_broadcast([P, G, HEADS, HD]),
                                ALU.mult).then_inc(s_vals, 1)
                fill_slot(at + BODY, r, s_slot1)

            with dve.If(1 - irregular(dve, DVE_ENGINE)):
                for r in range(RING):
                    fill_slot(r * G, r, s_slot1)
                dve.wait_ge(s_kvw[1], 16 * (CHUNKS // 2))
                dve.wait_ge(s_qcp, CHUNKS)
                for r in range(2):
                    make_onehot(r * G, r, 0, G, s_hot1)
                for r in range(RING):
                    group(r * G, r, r + 1, 16 * G, add_sums((r - 1) * G, r - 1, r, (r - 1) * G) if r else None, 3 * r)
                with dve.Fori(1, TURNS) as i:
                    for r in range(RING):
                        group(i * BODY + r * G, r, i * RING + (r + 1), i * (16 * G) + 16 * G,
                              add_sums(i * BODY + (r - 1) * G, (r - 1) % RING, i * RING + r, i * BODY + (r - 1) * G),
                              i * (3 * RING) + 3 * r)
                add = add_sums(TURNS * BODY - G, RING - 1, TURNS * RING, TURNS * BODY - G)
                for u in range(G):
                    add(u)
                dve.wait_ge(s_add1, TURNS * BODY + 1)
            with dve.If(irregular(dve, DVE_ENGINE)):
                e_score = e_prod[:, 0:HEADS]
                weight = e_state[:, D:W1]
                with dve.Fori(0, ORDERED_TILES * P) as n:
                    dve.wait_ge(s_load1, n * 64 + 64)
                    V.tensor_tensor(e_query, e_query, e_row[:, 0:D], ALU.mult).then_inc(s_one1, 1)
                    dve.wait_ge(s_one1, n * 5 + 1)
                    V.tensor_tensor(e_query, e_query, e_proj, ALU.mult).then_inc(s_one1, 1)
                    dve.wait_ge(s_one1, n * 5 + 2)
                    V.tensor_reduce(e_score, e_query.rearrange("p (h d) -> p h d", d=HD), AX.X, ALU.add).then_inc(s_one1, 1)
                    dve.wait_ge(s_one1, n * 5 + 3)
                    V.tensor_scalar(e_score, e_score, -CLIP, CLIP, ALU.max, ALU.min).then_inc(s_clip1, 1)
                    dve.wait_ge(s_eexp1, n + 1)
                    V.tensor_tensor(e_row[:, D:2 * D].rearrange("p (h d) -> p h d", d=HD),
                                    e_row[:, D:2 * D].rearrange("p (h d) -> p h d", d=HD),
                                    e_score.unsqueeze(2).to_broadcast([1, HEADS, HD]), ALU.mult).then_inc(s_one1, 1)
                    V.tensor_tensor(weight, weight, e_score, ALU.add).then_inc(s_one1, 1)
                    dve.wait_ge(s_one1, n * 5 + 5)
                    V.tensor_tensor(e_state[:, 0:D], e_state[:, 0:D], e_row[:, D:2 * D], ALU.add).then_inc(s_new1, 1)
                dve.wait_ge(s_back1, 16)

            def end_chunk(c, b, half, enters, norms, leaves):
                stats = aggregate = variance = nothing
                if norms:
                    stats, aggregate, variance = statistics(1 - b, c, s_y1, s_bn1, s_ag1, s_var1)
                if enters:
                    t = tiles(sums1, c * C, C)
                    n = c * 2
                    V.tensor_scalar(zr[:, b], t[:, :, D:W1], EPS_Z, None, ALU.add).then_inc(s_zch, 1)
                stats()
                if enters:
                    dve.wait_ge(s_zch, n + 1)
                    V.reciprocal(zr[:, b], zr[:, b]).then_inc(s_zch, 1)
                aggregate()
                if enters:
                    dve.wait_ge(s_zch, n + 2)
                    V.tensor_tensor(quot[b].rearrange("p k (h d) -> p k h d", d=HD),
                                    t[:, :, 0:D].rearrange("p k (h d) -> p k h d", d=HD),
                                    zr[:, b].unsqueeze(3).to_broadcast([P, C, HEADS, HD]), ALU.mult).then_inc(s_out1, 1)
                variance()
                if norms:
                    scales(1 - b, c, s_std1, s_rec1, s_scale1)
            chunk_loop(dve, end_chunk)


def kernel(x, src, dst, edge_attr_96, L0_gnn_W, L0_gnn_b, L1_gnn_Wq, L1_gnn_bq, L1_gnn_Wk, L1_gnn_bk,
           L1_gnn_We, L1_gnn_be, L1_gnn_Wv, L1_gnn_bv):
    import numpy as np
    import concourse.bacc as bacc
    from concourse.bass_utils import run_bass_kernel_spmd

    x, src, dst, edge, w0, b0, wq, bq, wk, bk, we, be, wv, bv = (
        np.asarray(a) for a in (x, src, dst, edge_attr_96, L0_gnn_W, L0_gnn_b, L1_gnn_Wq, L1_gnn_bq, L1_gnn_Wk,
                                L1_gnn_bk, L1_gnn_We, L1_gnn_be, L1_gnn_Wv, L1_gnn_bv))
    x_pad = np.concatenate([x, np.zeros((NT * P - NODES, D), x.dtype)])
    src = np.concatenate([src, np.zeros(ET * P - EDGES, src.dtype)]).reshape(ET, P)
    dst = np.concatenate([dst, np.full(ET * P - EDGES, NT * P - 1, dst.dtype)]).reshape(ET, P)
    edge = np.concatenate([edge, np.zeros((ET * P - EDGES, D), edge.dtype)])
    arrays = {
        "in_x": x_pad.reshape(NT, P, D).transpose(1, 0, 2),
        "in_ids": np.concatenate([src, dst], axis=1),
        "in_dst_last": dst[:, P - 1].reshape(1, ET),
        "in_dst_line": np.concatenate([dst.reshape(-1), dst[-1, -1:]]),
        "in_edge_t": edge.reshape(ET, P, D).transpose(0, 2, 1),
        "in_w0": np.concatenate([w0, b0[None]]),
        "in_wqkv": np.concatenate([np.concatenate([wq, wk, wv], axis=1), np.concatenate([bq, bk, bv])[None]]),
        "in_we": np.concatenate([we, be[None]]),
    }
    arrays = {k: np.ascontiguousarray(v) for k, v in arrays.items()}
    nc = bacc.Bacc("TRN2", target_bir_lowering=False, num_devices=1)
    aps = [nc.dram_tensor(k, v.shape, mybir.dt.from_np(v.dtype), kind="ExternalInput").ap()
           for k, v in arrays.items()]
    out = nc.dram_tensor("out", (P, NT, D), FP32, kind="ExternalOutput").ap()
    build(nc, *aps, out)
    got = run_bass_kernel_spmd(nc, [arrays], core_ids=[0]).results[0]["out"]
    return np.ascontiguousarray(got.transpose(1, 0, 2).reshape(NT * P, D)[:NODES])
```
